# Optimizing a Trainium2 kernel written in Bass

```python
import numpy as np
import jax
import jax.numpy as jnp

def _softmax(x, axis=-1):
    return jax.nn.softmax(x, axis=axis)

def _gelu(x):
    return jax.nn.gelu(x, approximate=True)

def _silu(x):
    return jax.nn.silu(x)

def _sigmoid(x):
    return jax.nn.sigmoid(x)

def _layernorm(x, axis=-1, eps=1e-05):
    m = jnp.mean(x, axis=axis, keepdims=True)
    v = jnp.var(x, axis=axis, keepdims=True)
    return (x - m) / jnp.sqrt(v + eps)

def _scatter_add(tgt, idx, src, axis=0):
    return tgt.at[idx].add(src)

def _segment_sum(src, seg, n):
    return jax.ops.segment_sum(src, seg, n)
kernel_name = 'mk_adaln_ffn_d2_seqx_r8_170805'

def setup_inputs(seed: int=0):
    np.random.seed(seed)
    _w = jnp.asarray

    def _rec_inputs():
        import jax
        import jax.numpy as jnp
        _rk = jax.random.key(seed)
        x = -0.000125 + 0.9999 * jax.random.normal(jax.random.fold_in(_rk, 1), (64, 32, 512), jnp.float32)
        _lenS = 32 - jax.random.randint(jax.random.fold_in(_rk, 7), (64,), 0, max(1, 32 // 4) + 1, jnp.int32)
        _lenS2 = 32 - jax.random.randint(jax.random.fold_in(_rk, 8), (64,), 0, max(1, 32 // 4) + 1, jnp.int32)
        itok_B_3_7 = jax.random.randint(jax.random.fold_in(_rk, 11), (64,), 3, 8, jnp.int32)
        itok_B_2_6 = jax.random.randint(jax.random.fold_in(_rk, 12), (64,), 2, 7, jnp.int32)
        return (x, itok_B_3_7, itok_B_2_6)
    x, itok_B_3_7, itok_B_2_6 = _rec_inputs()

    def _L0_cond_setup():
        import jax, jax.numpy as jnp
        import numpy as np
        MAX_LORAS, OUT, IN = (8, 512, 512)
        B, S = (4, 256)
        key = jax.random.key(seed)
        k1, k2, k3 = jax.random.split(key, 3)
        x = jax.random.normal(k1, (B, S, IN), dtype=jnp.float32)
        weight = jax.random.normal(k2, (MAX_LORAS, OUT, IN), dtype=jnp.float32) * 0.02
        adapter_ids = jax.random.randint(k3, (B,), 0, MAX_LORAS, dtype=jnp.int32)
        return {'x': x, 'weight': weight, 'adapter_ids': adapter_ids}
    _L0_cond_all = _L0_cond_setup()
    _L0_cond_in = {k: v for k, v in _L0_cond_all.items() if k in ('weight',)}
    del _L0_cond_all

    def _L0_ffn_setup():
        import jax, jax.numpy as jnp
        import numpy as np
        B, T, D_IN, D_OUT = (8, 256, 512, 512)
        N_LORAS, RANK = (16, 32)
        SCALING = 1.0
        key = jax.random.key(seed)
        ks = jax.random.split(key, 8)
        std = 1.0 / D_IN ** 0.5
        x = jax.random.normal(ks[0], (B, T, D_IN), dtype=jnp.float32)
        idx = jax.random.randint(ks[1], (B,), 0, N_LORAS)
        gate = jax.nn.one_hot(idx, N_LORAS, dtype=jnp.float32)
        kernel = jax.random.normal(ks[2], (D_IN, D_OUT), dtype=jnp.float32) * std
        bias = jnp.zeros((D_OUT,), dtype=jnp.float32)
        lora_A = jax.random.normal(ks[3], (N_LORAS, RANK, D_IN), dtype=jnp.float32) * std
        lora_B = jax.random.normal(ks[4], (N_LORAS, D_OUT, RANK), dtype=jnp.float32) * 0.01
        lora_A_shared = jax.random.normal(ks[5], (RANK, D_IN), dtype=jnp.float32) * std
        lora_B_shared = jax.random.normal(ks[6], (D_OUT, RANK), dtype=jnp.float32) * 0.01
        return {'x': x, 'gate': gate, 'kernel': kernel, 'bias': bias, 'lora_A': lora_A, 'lora_B': lora_B, 'lora_A_shared': lora_A_shared, 'lora_B_shared': lora_B_shared}
    _L0_ffn_all = _L0_ffn_setup()
    _L0_ffn_in = {k: v for k, v in _L0_ffn_all.items() if k in ('gate', 'kernel', 'bias', 'lora_A', 'lora_B', 'lora_A_shared', 'lora_B_shared')}
    del _L0_ffn_all

    def _L1_cond_setup():
        import jax, jax.numpy as jnp
        import numpy as np
        B, N, H, F = (4, 64, 512, 1376)
        L, R, RANK = (1, 16, 16)
        SCALE = 0.5
        key = jax.random.key(seed)
        ks = jax.random.split(key, 12)
        nrm = lambda k, shape, fan: jax.random.normal(k, shape, jnp.float32) * fan ** (-0.5)
        inp = {'x': jax.random.normal(ks[0], (B, N, H), jnp.float32), 'W_gate': nrm(ks[1], (F, H), H), 'W_up': nrm(ks[2], (F, H), H), 'W_down': nrm(ks[3], (H, F), F), 'A_gate': nrm(ks[4], (L, R, RANK, H), H), 'B_gate': nrm(ks[5], (L, R, F, RANK), RANK), 'A_up': nrm(ks[6], (L, R, RANK, H), H), 'B_up': nrm(ks[7], (L, R, F, RANK), RANK), 'A_down': nrm(ks[8], (L, R, RANK, F), F), 'B_down': nrm(ks[9], (L, R, H, RANK), RANK), 'lora_indices': jax.random.randint(ks[10], (B,), 0, R), 'layer_idx': 0}
        return inp
    _L1_cond_all = _L1_cond_setup()
    _L1_cond_in = {k: v for k, v in _L1_cond_all.items() if k in ('W_gate', 'W_up', 'W_down', 'A_gate', 'B_gate', 'A_up', 'B_up', 'A_down', 'B_down')}
    del _L1_cond_all

    def _L1_ffn_setup():
        import jax, jax.numpy as jnp
        import numpy as np
        RANKS = (8, 16, 32, 64)
        TOPK = 1
        SCALING = 1.0 / 4
        key = jax.random.key(seed)
        ks = jax.random.split(key, 7)
        D_IN, D_OUT, MAX_R, N_RANKS = (512, 512, 64, len(RANKS))
        B_, S_ = (4, 256)
        return {'hidden_states': jax.random.normal(ks[0], (B_, S_, D_IN), jnp.float32), 'W': jax.random.normal(ks[1], (D_OUT, D_IN), jnp.float32) * 0.02, 'b': jax.random.normal(ks[2], (D_OUT,), jnp.float32) * 0.02, 'A': jax.random.normal(ks[3], (MAX_R, D_IN), jnp.float32) * 0.02, 'B': jnp.zeros((D_OUT, MAX_R), jnp.float32) + jax.random.normal(ks[4], (D_OUT, MAX_R), jnp.float32) * 0.02, 'gate_w': jax.random.normal(ks[5], (N_RANKS, D_IN), jnp.float32) * 0.02, 'gate_b': jax.random.normal(ks[6], (N_RANKS,), jnp.float32) * 0.02}
    _L1_ffn_all = _L1_ffn_setup()
    _L1_ffn_in = {k: v for k, v in _L1_ffn_all.items() if k in ('W', 'b', 'A', 'B', 'gate_w', 'gate_b')}
    del _L1_ffn_all
    return {'x': x, 'itok_B_3_7': itok_B_3_7, 'itok_B_2_6': itok_B_2_6, 'L0_cond_weight': _L0_cond_in['weight'], 'L0_ffn_gate': _L0_ffn_in['gate'], 'L0_ffn_kernel': _L0_ffn_in['kernel'], 'L0_ffn_bias': _L0_ffn_in['bias'], 'L0_ffn_lora_A': _L0_ffn_in['lora_A'], 'L0_ffn_lora_B': _L0_ffn_in['lora_B'], 'L0_ffn_lora_A_shared': _L0_ffn_in['lora_A_shared'], 'L0_ffn_lora_B_shared': _L0_ffn_in['lora_B_shared'], 'L1_cond_W_gate': _L1_cond_in['W_gate'], 'L1_cond_W_up': _L1_cond_in['W_up'], 'L1_cond_W_down': _L1_cond_in['W_down'], 'L1_cond_A_gate': _L1_cond_in['A_gate'], 'L1_cond_B_gate': _L1_cond_in['B_gate'], 'L1_cond_A_up': _L1_cond_in['A_up'], 'L1_cond_B_up': _L1_cond_in['B_up'], 'L1_cond_A_down': _L1_cond_in['A_down'], 'L1_cond_B_down': _L1_cond_in['B_down'], 'L1_ffn_W': _L1_ffn_in['W'], 'L1_ffn_b': _L1_ffn_in['b'], 'L1_ffn_A': _L1_ffn_in['A'], 'L1_ffn_B': _L1_ffn_in['B'], 'L1_ffn_gate_w': _L1_ffn_in['gate_w'], 'L1_ffn_gate_b': _L1_ffn_in['gate_b']}

def reference(x, itok_B_3_7, itok_B_2_6, L0_cond_weight, L0_ffn_gate, L0_ffn_kernel, L0_ffn_bias, L0_ffn_lora_A, L0_ffn_lora_B, L0_ffn_lora_A_shared, L0_ffn_lora_B_shared, L1_cond_W_gate, L1_cond_W_up, L1_cond_W_down, L1_cond_A_gate, L1_cond_B_gate, L1_cond_A_up, L1_cond_B_up, L1_cond_A_down, L1_cond_B_down, L1_ffn_W, L1_ffn_b, L1_ffn_A, L1_ffn_B, L1_ffn_gate_w, L1_ffn_gate_b):
    import jax
    import jax.numpy as jnp

    def _L0_cond_ref(x, weight, adapter_ids):
        import jax, jax.numpy as jnp
        import numpy as np
        MAX_LORAS, OUT, IN = (8, 512, 512)
        B, S = (4, 256)
        w = weight[adapter_ids]
        return jnp.einsum('bsi,boi->bso', x, w)

    def _L0_ffn_ref(x, gate, kernel, bias, lora_A, lora_B, lora_A_shared, lora_B_shared):
        import jax, jax.numpy as jnp
        import numpy as np
        B, T, D_IN, D_OUT = (8, 256, 512, 512)
        N_LORAS, RANK = (16, 32)
        SCALING = 1.0
        base_out = jnp.matmul(x, kernel) + bias
        b = gate.shape[0]
        x_flat = x.reshape(b, -1, x.shape[-1])
        A_eff = jnp.einsum('bn,nri->bri', gate, lora_A)
        B_eff = jnp.einsum('bn,nor->bor', gate, lora_B)
        Ax = jnp.einsum('bri,bti->btr', A_eff, x_flat)
        delta_flat = jnp.einsum('bor,btr->bto', B_eff, Ax)
        Ax_s = jnp.einsum('ri,bti->btr', lora_A_shared, x_flat)
        delta_flat = delta_flat + jnp.einsum('or,btr->bto', lora_B_shared, Ax_s)
        delta = delta_flat.reshape(x.shape[:-1] + (kernel.shape[-1],))
        return base_out + (SCALING * delta).astype(base_out.dtype)

    def _L1_cond_ref(x, W_gate, W_up, W_down, A_gate, B_gate, A_up, B_up, A_down, B_down, lora_indices, layer_idx):
        import jax, jax.numpy as jnp
        import numpy as np
        B, N, H, F = (4, 64, 512, 1376)
        L, R, RANK = (1, 16, 16)
        SCALE = 0.5

        def lora_add(base, inp, A, B):
            Ab = A[layer_idx][lora_indices]
            Bb = B[layer_idx][lora_indices]
            t = jnp.einsum('bri,bni->bnr', Ab, inp)
            return base + jnp.einsum('bor,bnr->bno', Bb, t) * SCALE
        gate = lora_add(jnp.einsum('bnh,fh->bnf', x, W_gate), x, A_gate, B_gate)
        up = lora_add(jnp.einsum('bnh,fh->bnf', x, W_up), x, A_up, B_up)
        act = jax.nn.silu(gate) * up
        down = lora_add(jnp.einsum('bnf,hf->bnh', act, W_down), act, A_down, B_down)
        return down

    def _L1_ffn_ref(hidden_states, W, b, A, B, gate_w, gate_b):
        import jax, jax.numpy as jnp
        import numpy as np
        RANKS = (8, 16, 32, 64)
        TOPK = 1
        SCALING = 1.0 / 4
        bsz, seq, d_in = hidden_states.shape
        out = jnp.einsum('bsd,od->bso', hidden_states, W) + b
        x = hidden_states.reshape(-1, d_in)
        scores = x @ gate_w.T + gate_b
        probs = jax.nn.softmax(scores, axis=-1)
        routing_weights, selected = jax.lax.top_k(probs, TOPK)
        routing_weights = routing_weights / jnp.sum(routing_weights, axis=-1, keepdims=True)
        lora_outputs = jnp.stack([x @ A[:r, :].T @ B[:, :r].T for r in RANKS], axis=1)
        sel = jnp.take_along_axis(lora_outputs, selected[:, :, None], axis=1)
        final = jnp.sum(sel * routing_weights[:, :, None], axis=1)
        return out + final.reshape(bsz, seq, -1)
    x = x + _L0_ffn_ref(_L0_cond_ref(x, L0_cond_weight, itok_B_3_7), L0_ffn_gate, L0_ffn_kernel, L0_ffn_bias, L0_ffn_lora_A, L0_ffn_lora_B, L0_ffn_lora_A_shared, L0_ffn_lora_B_shared)
    x = x + _L1_ffn_ref(_L1_cond_ref(x, L1_cond_W_gate, L1_cond_W_up, L1_cond_W_down, L1_cond_A_gate, L1_cond_B_gate, L1_cond_A_up, L1_cond_B_up, L1_cond_A_down, L1_cond_B_down, itok_B_2_6, 0), L1_ffn_W, L1_ffn_b, L1_ffn_A, L1_ffn_B, L1_ffn_gate_w, L1_ffn_gate_b)
    return x

_drawn_inputs = setup_inputs


def setup_inputs(seed=0):
    import zlib

    import numpy as np

    out = dict(_drawn_inputs(seed))
    spreads = {'L0_ffn_bias': (0.0, 0.1)}
    factors = {'L1_ffn_b': 3.572, 'L1_ffn_gate_b': 25.065}
    for name, (base, spread) in spreads.items():
        noise = np.random.default_rng([zlib.crc32(name.encode()), seed]).standard_normal(out[name].shape)
        drawn = base * np.exp(spread * noise) if base else spread * noise
        out[name] = jnp.asarray(drawn.astype(out[name].dtype))
    for name, factor in factors.items():
        out[name] = (out[name] * factor).astype(out[name].dtype)
    return out
```

```python
from contextlib import ExitStack

import numpy as np

import concourse.bass as bass
from concourse import mybir

F32 = mybir.dt.float32
F32R = mybir.dt.float32r
I32 = mybir.dt.int32
U32 = mybir.dt.uint32
ACT = mybir.ActivationFunctionType
ALU = mybir.AluOpType
AX = mybir.AxisListType

P = 128
ITEMS, ITEM_T, D = 64, 32, 512
TOKENS = ITEMS * ITEM_T
C = D // P
N_COND = 8
GROUPS, N_LORA, RANK0 = 8, 16, 32
BI = 4
BT = BI * ITEM_T
NBLK = (ITEMS + N_COND * (BI - 1)) // BI
SLOTS = NBLK * BI
F = 1376
NF = -(-F // P)
N_ADP, RANK1 = 16, 16
GI = P // RANK1
GT = GI * ITEM_T
RANKS = (8, 16, 32, 64)
RMAX = RANKS[-1]
NR = len(RANKS)
RS = RMAX + NR
LINKS = 9 + NR
TB = 512
NTB = TOKENS // TB
NGT = TB // GT
SUB = TB // P
PREP_AT = 3
GPB = TB * GROUPS // TOKENS
R2 = GPB * RANK0
STAB = 3 * P
FIX = 3 * D

CONST_W = {
    "ident": P, "item_mask": GT, "group_mask": TB, "delta": RANK0, "ones": P, "before": ITEMS,
    "item_no": P, "adapter_no": N_COND, "fours": ITEMS // BI, "earlier": N_COND * N_COND, "slot_no": SLOTS,
    "dummy": SLOTS, "quadrant": BI, "row_in_item": 1, "chunk_row": NF + 1, "rank_row": 1,
}
CONST_AT = {}
_at = 0
for _k, _w in CONST_W.items():
    CONST_AT[_k] = _at
    _at += _w
CONST_N = _at


def constants():
    c = np.zeros((P, CONST_N), np.float32)

    def put(name, a):
        a = np.asarray(a, np.float32)
        a = a.reshape(a.shape[0], -1)
        c[:a.shape[0], CONST_AT[name]:CONST_AT[name] + a.shape[1]] = a

    p = np.arange(P)[:, None]
    put("ident", np.eye(P))
    put("item_mask", 0.5 * (p // RANK1 == np.arange(GT)[None] // ITEM_T))
    put("group_mask", p // RANK0 == np.arange(TB)[None] // (TOKENS // GROUPS))
    put("delta", p % RANK0 == np.arange(RANK0)[None])
    put("ones", np.ones((P, P)))
    put("before", np.arange(ITEMS)[:, None] < np.arange(ITEMS)[None])
    put("item_no", np.broadcast_to(np.arange(ITEMS)[:, None], (ITEMS, P)))
    put("adapter_no", np.broadcast_to(np.arange(N_COND), (P, N_COND)))
    put("fours", np.broadcast_to(BI * np.arange(ITEMS // BI), (P, ITEMS // BI)))
    e = np.arange(N_COND)
    put("earlier", np.broadcast_to((e[None] < e[:, None]).reshape(1, -1), (P, N_COND ** 2)))
    put("slot_no", np.broadcast_to(np.arange(SLOTS), (P, SLOTS)))
    put("dummy", np.broadcast_to(ITEMS + np.arange(SLOTS), (P, SLOTS)))
    put("quadrant", p // ITEM_T == np.arange(BI)[None])
    put("row_in_item", p % ITEM_T)
    put("chunk_row", np.broadcast_to(np.append(np.arange(NF) * N_ADP * RANK1, 0), (P, NF + 1)))
    put("rank_row", p % RANK1)
    return c


def two_layers(nc, a, out):
    with ExitStack() as ctx:
        base = -(-nc.sbuf_base // 64) * 64
        top = {"at": base}

        def sb(name, shape, dt, at=None):
            size = 4 * int(np.prod(shape[1:]))
            if at is None:
                at = top["at"]
                top["at"] = at + -(-size // 32) * 32
            return nc.alloc_sbuf_tensor_at(name, list(shape), dt, offset=at)

        def pair(name, shape):
            return sb(name + "_hi", shape, F32R), sb(name + "_lo", shape, F32R)

        def psum(name, shape):
            return ctx.enter_context(nc.psum_tensor(name, list(shape), F32))

        def sem(name):
            return ctx.enter_context(nc.semaphore(name))

        const = sb("const", [P, CONST_N], F32)
        bias = sb("bias", [P, 2 * C + 1], F32)
        k_hi, k_lo = pair("kern", [P, C, D])
        a_eff = sb("a_eff", [P, C, GROUPS * RANK0], F32)
        b_eff = sb("b_eff", [R2, NTB, D], F32)
        wf_at = top["at"]
        wf_raw = sb("wf_raw", [P, C, D], F32)
        wf_lo = sb("wf_lo", [P, C, D], F32R, at=wf_at)
        ra_at = top["at"]
        ra_raw = sb("ra_raw", [P, C, RS], F32)
        ra_lo = sb("ra_lo", [P, C, RS], F32R, at=ra_at)
        rb_at = top["at"]
        rb_raw = sb("rb_raw", [RMAX, D], F32)
        rb_lo = sb("rb_lo", [RMAX, D], F32R, at=rb_at)
        idx_tab = sb("idx_tab", [P, ITEMS // GI, NF + 1], U32)
        shared_from = top["at"]

        w_hi, w_lo = pair("cond_w", [P, N_COND, C * D])
        w_raw = sb("w_raw", [P, 2, D * C // 2], F32)
        xs = sb("xs", [P, 2, D], F32)
        xs_hi, xs_lo = pair("xs_t", [P, 2, D])
        h0 = sb("h0", [P, 2, D], F32)
        cond_end = top["at"]
        w_part = 4 * C * D
        top["at"] = shared_from + PREP_AT * w_part
        lora = sb("lora", [P, 2, 4, D], F32)
        lora_hi = sb("lora_hi", [P, 2, 4, D], F32R)
        kraw = sb("kraw", [P, C, D], F32)
        assert top["at"] <= shared_from + N_COND * w_part
        top["at"] = shared_from + (N_COND + PREP_AT) * w_part
        lora_lo = sb("lora_lo", [P, 2, 4, D], F32R)
        gsel = sb("gsel", [P, 4, GROUPS * RANK0], F32)
        g_hi, g_lo = pair("gsel_s", [P, 4, GROUPS * RANK0])
        sh = sb("shared", [RANK0, 2, D], F32)
        sh_hi, sh_lo = pair("shared_s", [RANK0, 2, D])
        assert top["at"] <= shared_from + 2 * N_COND * w_part
        top["at"] = cond_end
        gate_v = sb("gate_v", [P, 4, GROUPS], F32)
        ids0 = sb("ids0", [ITEMS, 1], I32)
        ids0f = sb("ids0f", [ITEMS, 1], F32)
        ids1 = sb("ids1", [P, GROUPS], I32)
        ids1f = sb("ids1f", [P, GROUPS], F32)
        onehot = sb("onehot", [ITEMS, N_COND], F32)
        over = sb("over", [ITEMS, N_COND, ITEMS // BI], F32)
        nblk = sb("nblk", [ITEMS, N_COND], F32)
        earlier = sb("earlier_n", [ITEMS, N_COND, N_COND], F32)
        start = sb("start", [ITEMS, N_COND], F32)
        place = sb("place", [ITEMS, N_COND], F32)
        own = sb("own", [ITEMS, N_COND], F32)
        slot = sb("slot", [ITEMS, 1], F32)
        perm = sb("perm", [ITEMS, SLOTS], F32)
        item_g = sb("item_g", [P, SLOTS], F32)
        empty = sb("empty", [P, SLOTS], F32)
        dummy = sb("dummy_s", [P, SLOTS], F32)
        item_s = sb("item_s", [P, SLOTS], F32)
        sel_g = sb("sel_g", [P, NBLK, BI], F32)
        sel_s = sb("sel_s", [P, NBLK, BI], F32)
        row_g = sb("row_g", [P, NBLK], F32)
        row_s = sb("row_s", [P, NBLK], F32)
        idx_base = sb("idx_base", [P, GROUPS], F32)
        idx_g = sb("idx_g", [P, NBLK], U32)
        idx_s = sb("idx_s", [P, NBLK], U32)
        idx_gn = sb("idx_gn", [P, 2], U32)
        idx_sn = sb("idx_sn", [P, 2], U32)
        blk_adp = sb("blk_adp", [1, SLOTS], I32)
        cond_top = top["at"]
        assert cond_top <= nc.sbuf_usable_end

        top["at"] = shared_from
        wf_hi = sb("wf_hi", [P, C, D], F32R)
        ra_hi = sb("ra_hi", [P, C, RS], F32R)
        rb_hi = sb("rb_hi", [RMAX, D], F32R)
        tok_at = top["at"]
        tok = sb("tok", [P, SUB, D], F32)
        tokf = sb("x_t", [P, C, TB], F32, at=tok_at)
        ht_hi, ht_lo = pair("ht", [P, C, TB])
        x1_hi, x1_lo = pair("x1", [P, C, TB])
        ae_hi, ae_lo = pair("ae", [P, C, R2])
        r64_hi, r64_lo = pair("r64", [RMAX, TB])
        fix = sb("fix", [P, NGT, FIX], F32)
        at_hi, at_lo = pair("at", [P, 2, D])
        tm = sb("tm", [P, TB], F32)
        tg_at = top["at"]
        tg_hi, tg_lo = pair("tg", [P, 2, TB])
        be_at = top["at"]
        td_hi, td_lo = pair("td", [P, TB])
        be_hi = sb("be_hi", [R2, D], F32R, at=be_at)
        be_lo = sb("be_lo", [R2, D], F32R, at=be_at + 4 * TB)
        bd_hi, bd_lo = pair("bd", [P, NGT, D])
        gu_raw = sb("gu_raw", [P, 2 * D], F32)
        gu_hi, gu_lo = pair("gu", [P, 2, 2 * D])
        dn_raw = sb("dn_raw", [P, D], F32)
        dn_hi, dn_lo = pair("dn", [P, 2, D])
        ab = sb("ab", [P, 2, NGT, STAB], F32)
        bu_hi, bu_lo = pair("bu", [P, 2, NGT, 2 * P])
        ad_hi, ad_lo = pair("ad", [P, 2, NGT * P])
        scores_at = top["at"]
        silu = sb("silu", [P, TB], F32)
        r64_at = top["at"]
        act_f = sb("act_f", [P, TB], F32)
        act_hi, act_lo = pair("act", [P, 2, TB])
        idx_blk = sb("idx_blk", [P, NGT, NF + 1], U32)
        idx_row = sb("idx_row", [P, 2, NGT], U32)
        scores = sb("scores", [RS, TB], F32, at=scores_at)
        r64 = sb("r64", [RMAX, TB], F32, at=r64_at)
        soft = sb("soft", [P, 12, SUB, NR], F32)
        mexp = sb("mexp", [P, SUB, RMAX], F32)
        main_top = top["at"]
        assert main_top <= nc.sbuf_usable_end
        ob = sb("out_b", [P, C, TB], F32, at=tg_at)

        psD = psum("psD", [P, 4, TB])
        psT = psum("psT", [P, TB])
        psG = psum("psG", [P, TB])
        psU = psum("psU", [P, TB])
        psX = psum("psX", [P, TB])

        def cst(name, rows=P):
            return const[0:rows, CONST_AT[name]:CONST_AT[name] + CONST_W[name]]

        h0_dram = nc.dram_tensor("h0_scratch", [TOKENS + SLOTS * ITEM_T, D], F32, kind="Internal").ap()

        names = """const_in small_in lora_in kraw_in late_in w_in0 w_in1
            ids_f sort_v sort_ps1 sort_ps2 idx_ready idx_tab_ready
            gsel_f prep_hi prep_lo kern_ps kern_f kern_hi kern_lo aeff_ps beff_ps aeff_done beff_done
            w_hi_s w_lo_s0 w_lo_s1 xs_in0 xs_in1 xs_ps0 xs_ps1 xs_hi0 xs_hi1 xs_lo0 xs_lo1 h_ps0 h_ps1 h_out0 h_out1
            h_st0 h_st1
            wf_hi_s wf_lo_s
            h0_in h0t_ps h0t_hi h0t_lo ae_s be_s ae_l be_l x_in t0_ps t0_m t0_hi t0_lo x1_ps x1_f x1_hi_s x1_lo_s
            idx_b fix_in at_ps at_hi_s at_lo_s tg_ps tg_m tg_hi_s tg_lo_s bd_hi_s bd_lo_s
            idx_r idx_gn0 idx_gn1 idx_sn0 idx_sn1 gu_in dn_in ab_in0 ab_in1 gu_hi_s gu_lo_s bu_hi_s bu_lo_s dn_hi_s dn_lo_s
            ad_ps ad_hi_s ad_lo_s gate_ps up_ps silu_s act_f_s act_hi_s act_lo_s td_ps dn_ps
            td_m td_hi_s td_lo_s h_ps h_hi_s h_lo_s r_ps r_sb sc_ps sc_v exp_s soft_v mexp_s mask_ps
            xa_m xa_hi xa_lo out_ps out_v out_f out_st""".split()
        S = {n: sem(n) for n in names}

        block = ctx.enter_context(nc.Block())

        def value(eng, count):
            return count if isinstance(count, int) else eng.to_reg(count)

        def alone(eng):
            eng.wait_ge(S["const_in"], 16)

        def last(fc, before=0):
            return isinstance(fc, int) and fc == NF - 1 - before


        def chunks(eng, body, head, tail):
            pairs = (NF - head - tail) // 2
            for fc in range(head):
                body(fc, fc // 2, fc % 2)
            with eng.Fori(0, pairs) as i:
                for k in (head, head + 1):
                    body(2 * i + k, i + k // 2, k % 2)
            for fc in range(head + 2 * pairs, NF):
                body(fc, fc // 2, fc % 2)

        @block.sync
        def _(sp):
            sp.dma_start(const[:], a["const"]).then_inc(S["const_in"], 16)
            sp.dma_start(ids0[:], a["ids0"]).then_inc(S["small_in"], 16)
            sp.dma_start(ids1[:], a["ids1"]).then_inc(S["small_in"], 16)
            sp.dma_start(gate_v[:], a["gate"]).then_inc(S["small_in"], 16)
            sp.dma_start(bias[:], a["bias"]).then_inc(S["small_in"], 16)
            sp.dma_start(sh[:], a["shared"]).then_inc(S["small_in"], 16)
            sp.dma_start(lora[:], a["lora"]).then_inc(S["lora_in"], 16)
            sp.dma_start(kraw[:], a["kern"]).then_inc(S["kraw_in"], 16)
            with sp.Fori(0, N_COND) as e:
                for h in range(2):
                    sp.wait_ge(S[f"w_lo_s{h}"], e)
                    sp.dma_start(w_raw[:, h, :], a["cond_w"][bass.ds(e, 1), :, h * C * D // 2:(h + 1) * C * D // 2]
                                 .rearrange("e p n -> (e p) n")).then_inc(S[f"w_in{h}"], 16)
            sp.dma_start(wf_raw[:], a["wf"]).then_inc(S["late_in"], 16)
            sp.dma_start(ra_raw[:], a["ra"]).then_inc(S["late_in"], 16)
            sp.dma_start(rb_raw[:], a["rb"]).then_inc(S["late_in"], 16)
            sp.wait_ge(S["h_st0"], 16 * ((NBLK + 1) // 2))
            sp.wait_ge(S["h_st1"], 16 * (NBLK // 2))
            with sp.Fori(0, NTB) as t:
                sp.wait_ge(S["x1_hi_s"], C * t)
                sp.wait_ge(S["x1_lo_s"], C * t)
                sp.dma_start(tok[:], h0_dram[bass.ds(t * TB, TB), :].rearrange("(s p) d -> p s d", p=P)
                             ).then_inc(S["h0_in"], 16)
                sp.wait_ge(S["h0t_ps"], C * t + C)
                sp.dma_start(tokf[:], a["x_t"][bass.ds(t, 1), :, :].rearrange("t p (c n) -> (t p) c n", c=C)
                             ).then_inc(S["x_in"], 16)

                def load(fc, j, par):
                    n = NF * t + fc
                    sp.wait_ge(S["gu_hi_s"], n)
                    sp.wait_ge(S["gu_lo_s"], n)
                    sp.dma_start(gu_raw[:], a["gu"][bass.ds(fc, 1), :, :].rearrange("f p n -> (f p) n")
                                 ).then_inc(S["gu_in"], 16)
                    sp.wait_ge(S["dn_hi_s"], n)
                    sp.wait_ge(S["dn_lo_s"], n)
                    sp.dma_start(dn_raw[:], a["dn"][bass.ds(fc, 1), :, :].rearrange("f p n -> (f p) n")
                                 ).then_inc(S["dn_in"], 16)

                chunks(sp, load, 0, 1)

        @block.gpsimd
        def _(pool):
            def low(dst, x, hi, s):
                pool.tensor_tensor(dst, x, hi, ALU.subtract).then_inc(s, 1)

            pool.wait_ge(S["const_in"], 16)
            pool.wait_ge(S["small_in"], 80)
            pool.tensor_tensor(gsel[:].rearrange("p k (g r) -> p (k g) r", r=RANK0),
                               cst("delta").unsqueeze(1).broadcast_to([P, 4 * GROUPS, RANK0]),
                               gate_v[:].rearrange("p k g -> p (k g)").unsqueeze(2).broadcast_to([P, 4 * GROUPS, RANK0]),
                               ALU.mult).then_inc(S["gsel_f"], 1)
            pool.wait_ge(S["prep_hi"], 1)
            low(sh_lo[:], sh[:], sh_hi[:], S["prep_lo"])
            pool.wait_ge(S["prep_hi"], 2)
            low(g_lo[:], gsel[:], g_hi[:], S["prep_lo"])
            pool.wait_ge(S["prep_hi"], 3)
            low(lora_lo[:], lora[:], lora_hi[:], S["prep_lo"])
            pool.wait_ge(S["kern_f"], C)
            pool.wait_ge(S["kern_hi"], 1)
            low(k_lo[:], kraw[:], k_hi[:], S["kern_lo"])

            def gather(par, b, it):
                count0 = value(pool, it)
                alone(pool)
                pool.wait_ge(S[f"xs_ps{par}"], count0)
                pool.tensor_copy(idx_gn[:, par:par + 1], idx_g[:, bass.ds(b, 1)]).then_inc(S[f"idx_gn{par}"], 1)
                count0 = value(pool, it + 1)
                alone(pool)
                pool.wait_ge(S[f"idx_gn{par}"], count0)
                pool.indirect_dma_start(xs[:, par, :], None, a["x"],
                                        bass.IndirectOffsetOnAxis(idx_gn[:, par:par + 1], 0)
                                        ).then_inc(S[f"xs_in{par}"], 16)

            def scatter(par, b, it):
                count0 = value(pool, it + 1)
                alone(pool)
                pool.wait_ge(S[f"h_out{par}"], count0)
                pool.tensor_copy(idx_sn[:, par:par + 1], idx_s[:, bass.ds(b, 1)]).then_inc(S[f"idx_sn{par}"], 1)
                count0 = value(pool, it + 1)
                alone(pool)
                pool.wait_ge(S[f"idx_sn{par}"], count0)
                pool.indirect_dma_start(h0_dram, bass.IndirectOffsetOnAxis(idx_sn[:, par:par + 1], 0),
                                        h0[:, par, :], None).then_inc(S[f"h_st{par}"], 16)

            pool.wait_ge(S["idx_ready"], 1)
            gather(0, 0, 0)
            gather(1, 1, 0)
            with pool.Fori(0, NBLK // 2 - 1) as it:
                scatter(0, 2 * it, it)
                gather(0, 2 * it + 2, it + 1)
                scatter(1, 2 * it + 1, it)
                gather(1, 2 * it + 3, it + 1)
            scatter(0, NBLK - 2, NBLK // 2 - 1)
            scatter(1, NBLK - 1, NBLK // 2 - 1)

            pool.wait_ge(S["wf_hi_s"], 1)
            low(wf_lo[:], wf_raw[:], wf_hi[:], S["wf_lo_s"])
            pool.wait_ge(S["wf_hi_s"], 2)
            low(ra_lo[:], ra_raw[:], ra_hi[:], S["wf_lo_s"])
            pool.wait_ge(S["wf_hi_s"], 3)
            low(rb_lo[:], rb_raw[:], rb_hi[:], S["wf_lo_s"])
            pool.wait_ge(S["h_st0"], 16 * ((NBLK + 1) // 2))
            pool.wait_ge(S["h_st1"], 16 * (NBLK // 2))
            pool.wait_ge(S["idx_tab_ready"], 1)

            with pool.Fori(0, NTB) as t:
                count0 = value(pool, 16 * NGT * (NF // 2 + 1) * t)
                count1 = value(pool, 16 * NGT * (NF // 2) * t)
                count2 = value(pool, 16 * NGT * t)
                alone(pool)
                pool.wait_ge(S["ab_in0"], count0)
                pool.wait_ge(S["ab_in1"], count1)
                pool.wait_ge(S["fix_in"], count2)
                pool.tensor_copy(idx_blk[:], idx_tab[:, bass.ds(t * NGT, NGT), :]).then_inc(S["idx_b"], 1)
                count0 = value(pool, t + 1)
                count1 = value(pool, 4 * t)
                count2 = value(pool, t)
                count3 = value(pool, t)
                alone(pool)
                pool.wait_ge(S["idx_b"], count0)
                pool.wait_ge(S["at_ps"], count1)
                pool.wait_ge(S["bd_hi_s"], count2)
                pool.wait_ge(S["bd_lo_s"], count3)
                for g in range(NGT):
                    pool.indirect_dma_start(fix[:, g, :], None, a["fix"],
                                            bass.IndirectOffsetOnAxis(idx_blk[:, g, NF:NF + 1], 0)
                                            ).then_inc(S["fix_in"], 16)

                def rows(fc, par, n):
                    pool.tensor_copy(idx_row[:, par, :].unsqueeze(2), idx_blk[:, :, bass.ds(fc, 1)]
                                     ).then_inc(S["idx_r"], 1)
                    count0 = value(pool, n + 1)
                    alone(pool)
                    pool.wait_ge(S["idx_r"], count0)
                    for g in range(NGT):
                        pool.indirect_dma_start(ab[:, par, g, :], None, a["ab"],
                                                bass.IndirectOffsetOnAxis(idx_row[:, par, g:g + 1], 0)
                                                ).then_inc(S[f"ab_in{par}"], 16)

                def low_gu(par, n):
                    pool.wait_ge(S["gu_hi_s"], n + 1)
                    low(gu_lo[:, par, :], gu_raw[:], gu_hi[:, par, :], S["gu_lo_s"])
                    pool.wait_ge(S["bu_hi_s"], n + 1)
                    low(bu_lo[:, par], ab[:, par, :, P:STAB], bu_hi[:, par], S["bu_lo_s"])

                count0 = value(pool, NF * t)
                count1 = value(pool, NF * t)
                count2 = value(pool, NF * t)
                alone(pool)
                pool.wait_ge(S["bu_hi_s"], count0)
                pool.wait_ge(S["bu_lo_s"], count1)
                pool.wait_ge(S["ad_ps"], count2)
                rows(0, 0, NF * t)
                rows(1, 1, NF * t + 1)
                pool.wait_ge(S["ae_s"], t + 1)
                low(ae_lo[:], a_eff[:, :, bass.ds(t * R2, R2)], ae_hi[:], S["ae_l"])
                pool.wait_ge(S["be_s"], t + 1)
                low(be_lo[:].unsqueeze(1), b_eff[:, bass.ds(t, 1), :], be_hi[:].unsqueeze(1), S["be_l"])
                low_gu(0, NF * t)
                pool.wait_ge(S["bd_hi_s"], t + 1)
                low(bd_lo[:], fix[:, :, 2 * D:FIX], bd_hi[:], S["bd_lo_s"])

                def step(fc, j, par):
                    n = NF * t + fc
                    if not last(fc):
                        low_gu(1 - par, n + 1)
                    pool.wait_ge(S["dn_hi_s"], n + 1)
                    low(dn_lo[:, par, :], dn_raw[:], dn_hi[:, par, :], S["dn_lo_s"])
                    if not last(fc) and not last(fc, 1):
                        count0 = value(pool, n + 1)
                        count1 = value(pool, n + 1)
                        count2 = value(pool, n + 1)
                        alone(pool)
                        pool.wait_ge(S["bu_hi_s"], count0)
                        pool.wait_ge(S["bu_lo_s"], count1)
                        pool.wait_ge(S["ad_ps"], count2)
                        rows(fc + 2, par, n + 2)

                chunks(pool, step, 1, 2)

        @block.scalar
        def _(act):
            def high(dst, x, s):
                act.activation(dst, x, ACT.Copy).then_inc(s, 1)

            act.wait_ge(S["small_in"], 80)
            high(sh_hi[:], sh[:], S["prep_hi"])
            act.wait_ge(S["gsel_f"], 1)
            high(g_hi[:], gsel[:], S["prep_hi"])
            act.wait_ge(S["lora_in"], 16)
            high(lora_hi[:], lora[:], S["prep_hi"])
            act.wait_ge(S["kern_f"], C)
            high(k_hi[:], kraw[:], S["kern_hi"])
            for j in range(2):
                act.wait_ge(S["aeff_ps"], j + 1)
                act.activation(a_eff[:, 2 * j:2 * j + 2, :],
                               (psG if j == 0 else psU)[:].rearrange("p (c n) -> p c n", c=2), ACT.Copy
                               ).then_inc(S["aeff_done"], 1)
            for j in range(NTB):
                act.wait_ge(S["beff_ps"], j + 1)
                act.activation(b_eff[:, j, :], psD[0:R2, j, :], ACT.Copy).then_inc(S["beff_done"], 1)

            with act.Fori(0, NBLK // 2) as it:
                for par in range(2):
                    act.wait_ge(S[f"xs_ps{par}"], it + 1)
                    act.wait_ge(S[f"h_ps{par}"], it)
                    act.activation(xs_hi[:, par, :], (psG, psU)[par][:], ACT.Copy).then_inc(S[f"xs_hi{par}"], 1)
                    act.wait_ge(S[f"h_ps{par}"], it + 1)
                    act.wait_ge(S[f"h_st{par}"], 16 * it)
                    act.activation(h0[:, par, :], (psT, psX)[par][:], ACT.Copy).then_inc(S[f"h_out{par}"], 1)

            act.wait_ge(S["h_st0"], 16 * ((NBLK + 1) // 2))
            act.wait_ge(S["h_st1"], 16 * (NBLK // 2))
            act.wait_ge(S["late_in"], 48)
            high(wf_hi[:], wf_raw[:], S["wf_hi_s"])
            high(ra_hi[:], ra_raw[:], S["wf_hi_s"])
            high(rb_hi[:], rb_raw[:], S["wf_hi_s"])

            with act.Fori(0, NTB) as t:
                act.wait_ge(S["x1_ps"], C * t)
                high(ae_hi[:], a_eff[:, :, bass.ds(t * R2, R2)], S["ae_s"])
                for c in range(C):
                    act.wait_ge(S["h0t_ps"], C * t + c + 1)
                    high(ht_hi[:, c, :], psD[:, c, :], S["h0t_hi"])
                high(be_hi[:].unsqueeze(1), b_eff[:, bass.ds(t, 1), :], S["be_s"])
                act.wait_ge(S["at_ps"], 4 * t + 1)
                high(at_hi[:, 0, :], psX[:], S["at_hi_s"])
                act.wait_ge(S["t0_m"], t + 1)
                high(r64_hi[:], r64[:], S["t0_hi"])

                def high_gu(par, n, free, gathers):
                    act.wait_ge(S["gu_in"], 16 * (n + 1))
                    act.wait_ge(S["up_ps"], free)
                    high(gu_hi[:, par, :], gu_raw[:], S["gu_hi_s"])
                    act.wait_ge(S[f"ab_in{par}"], 16 * NGT * gathers)
                    high(bu_hi[:, par], ab[:, par, :, P:STAB], S["bu_hi_s"])

                high_gu(0, NF * t, NF * t, (NF // 2 + 1) * t + 1)
                act.wait_ge(S["fix_in"], 16 * NGT * (t + 1))
                act.wait_ge(S["h_ps"], C * t)
                high(bd_hi[:], fix[:, :, 2 * D:FIX], S["bd_hi_s"])
                for o in range(C):
                    act.wait_ge(S["x1_f"], C * t + o + 1)
                    high(x1_hi[:, o, :], tokf[:, o, :], S["x1_hi_s"])
                for k in range(1, 4):
                    act.wait_ge(S["at_ps"], 4 * t + k + 1)
                    high(at_hi[:, k % 2, :], (psX, psT)[k % 2][:], S["at_hi_s"])
                act.wait_ge(S["out_st"], 16 * t)
                for k in range(2):
                    act.wait_ge(S["tg_m"], 2 * t + k + 1)
                    high(tg_hi[:, k, :], tm[:], S["tg_hi_s"])

                def step(fc, j, par):
                    n = NF * t + fc
                    if not last(fc):
                        high_gu(1 - par, n + 1, n, (NF // 2 + par) * t + j + par + 1)
                    act.wait_ge(S["ad_ps"], n + 1)
                    act.wait_ge(S["dn_ps"], n if isinstance(fc, int) and fc == 0 else n - 1)
                    high(ad_hi[:, par, :], psX[:, 0:NGT * P], S["ad_hi_s"])
                    act.wait_ge(S["dn_in"], 16 * (n + 1))
                    high(dn_hi[:, par, :], dn_raw[:], S["dn_hi_s"])
                    act.wait_ge(S["gate_ps"], n + 1)
                    act.wait_ge(S["act_f_s"], n)
                    act.activation(silu[:], psG[:], ACT.Silu).then_inc(S["silu_s"], 1)
                    act.wait_ge(S["act_f_s"], n + 1)
                    high(act_hi[:, par, :], act_f[:], S["act_hi_s"])

                chunks(act, step, 1, 1)

                act.wait_ge(S["td_m"], t + 1)
                high(td_hi[:], tm[:], S["td_hi_s"])
                for o in range(C):
                    act.wait_ge(S["h_ps"], C * t + o + 1)
                    high(ht_hi[:, o, :], psD[:, o, :], S["h_hi_s"])
                act.wait_ge(S["r_ps"], t + 1)
                act.activation(scores[RMAX:RS, :], psX[RMAX:RS, :], ACT.Identity,
                               bias=bias[RMAX:RS, 2 * C:2 * C + 1]).then_inc(S["r_sb"], 1)
                act.activation(scores[0:RMAX, :], psX[0:RMAX, :], ACT.Copy).then_inc(S["r_sb"], 1)
                act.wait_ge(S["sc_v"], t + 1)
                act.activation(soft[:, 2], soft[:, 1], ACT.Exp).then_inc(S["exp_s"], 1)
                act.wait_ge(S["xa_m"], t + 1)
                high(r64_hi[:], r64[:], S["xa_hi"])
                act.wait_ge(S["out_f"], C * (t + 1))
                act.dma_start(out[bass.ds(t, 1), :, :].rearrange("t p (c n) -> (t p) c n", c=C), ob[:]
                              ).then_inc(S["out_st"], 16)
            act.wait_ge(S["out_st"], 16 * NTB)

        @block.vector
        def _(dve):
            def low(dst, x, hi, s):
                dve.tensor_tensor(dst, x, hi, ALU.subtract).then_inc(s, 1)

            done = [0]

            def then(ins):
                done[0] += 1
                ins.then_inc(S["sort_v"], 1)
                dve.wait_ge(S["sort_v"], done[0])

            dve.wait_ge(S["const_in"], 16)
            dve.wait_ge(S["small_in"], 80)
            then(dve.tensor_copy(ids0f[:], ids0[:]))
            dve.tensor_scalar(onehot[:], cst("adapter_no", ITEMS), ids0f[:], None, ALU.is_equal
                              ).then_inc(S["ids_f"], 1)
            then(dve.tensor_copy(ids1f[:], ids1[:]))
            then(dve.tensor_scalar(idx_base[:], ids1f[:], float(RANK1), cst("rank_row"), ALU.mult, ALU.add))
            dve.tensor_tensor(idx_tab[:], idx_base[:].unsqueeze(2).broadcast_to([P, GROUPS, NF + 1]),
                              cst("chunk_row").unsqueeze(1).broadcast_to([P, GROUPS, NF + 1]), ALU.add
                              ).then_inc(S["idx_tab_ready"], 1)
            dve.wait_ge(S["sort_ps1"], 1)
            then(dve.tensor_tensor(over[:], psX[0:ITEMS, N_COND:2 * N_COND].unsqueeze(2)
                                   .broadcast_to([ITEMS, N_COND, ITEMS // BI]),
                                   cst("fours", ITEMS).unsqueeze(1).broadcast_to([ITEMS, N_COND, ITEMS // BI]),
                                   ALU.is_gt))
            then(dve.tensor_reduce(nblk[:], over[:], AX.X, ALU.add))
            then(dve.tensor_tensor(earlier[:], nblk[:].unsqueeze(1).broadcast_to([ITEMS, N_COND, N_COND]),
                                   cst("earlier", ITEMS).rearrange("p (a b) -> p a b", a=N_COND), ALU.mult))
            then(dve.tensor_reduce(start[:], earlier[:], AX.X, ALU.add))
            then(dve.scalar_tensor_tensor(out=place[:], in0=start[:], scalar=float(BI), in1=psX[0:ITEMS, 0:N_COND],
                                          op0=ALU.mult, op1=ALU.add))
            then(dve.tensor_tensor(own[:], place[:], onehot[:], ALU.mult))
            then(dve.tensor_reduce(slot[:], own[:], AX.X, ALU.add))
            then(dve.tensor_scalar(perm[:], cst("slot_no", ITEMS), slot[:], None, ALU.is_equal))
            dve.wait_ge(S["sort_ps2"], 1)
            dve.tensor_copy(blk_adp[:], psX[0:1, 2 * SLOTS:3 * SLOTS])
            then(dve.tensor_copy(item_g[:], psX[:, 0:SLOTS]))
            then(dve.tensor_scalar(empty[:], psX[:, SLOTS:2 * SLOTS], -1.0, 1.0, ALU.mult, ALU.add))
            then(dve.tensor_tensor(dummy[:], empty[:], cst("dummy"), ALU.mult))
            then(dve.tensor_tensor(item_s[:], item_g[:], dummy[:], ALU.add))
            quad = cst("quadrant").unsqueeze(1).broadcast_to([P, NBLK, BI])
            dve.tensor_tensor(sel_g[:], item_g[:].rearrange("p (b j) -> p b j", j=BI), quad, ALU.mult)
            then(dve.tensor_tensor(sel_s[:], item_s[:].rearrange("p (b j) -> p b j", j=BI), quad, ALU.mult))
            dve.tensor_reduce(row_g[:], sel_g[:], AX.X, ALU.add)
            then(dve.tensor_reduce(row_s[:], sel_s[:], AX.X, ALU.add))
            dve.tensor_scalar(idx_g[:], row_g[:], float(ITEM_T), cst("row_in_item"), ALU.mult, ALU.add)
            dve.tensor_scalar(idx_s[:], row_s[:], float(ITEM_T), cst("row_in_item"), ALU.mult, ALU.add
                              ).then_inc(S["idx_ready"], 1)
            dve.wait_ge(S["kraw_in"], 16)
            for c in range(C):
                dve.wait_ge(S["kern_ps"], c + 1)
                dve.tensor_tensor(kraw[:, c, :], psD[:, c, :], kraw[:, c, :], ALU.add).then_inc(S["kern_f"], 1)

            def split_w(e, h):
                dve.wait_ge(S[f"w_in{h}"], 16 * e + 16)
                v = w_hi[:, bass.ds(e, 1), h * C * D // 2:(h + 1) * C * D // 2]
                dve.tensor_copy(v, w_raw[:, h:h + 1, :]).then_inc(S["w_hi_s"], 1)
                dve.wait_ge(S["w_hi_s"], 2 * e + h + 1)
                dve.tensor_tensor(w_lo[:, bass.ds(e, 1), h * C * D // 2:(h + 1) * C * D // 2], w_raw[:, h:h + 1, :], v,
                                  ALU.subtract).then_inc(S[f"w_lo_s{h}"], 1)

            with dve.Fori(0, PREP_AT) as e:
                for h in range(2):
                    split_w(e, h)
            dve.wait_ge(S["beff_done"], NTB)
            dve.wait_ge(S["kern_lo"], 1)
            with dve.Fori(PREP_AT, N_COND) as e:
                for h in range(2):
                    split_w(e, h)

            with dve.Fori(0, NBLK // 2) as it:
                for par in range(2):
                    dve.wait_ge(S[f"xs_hi{par}"], it + 1)
                    low(xs_lo[:, par, :], (psG, psU)[par][:], xs_hi[:, par, :], S[f"xs_lo{par}"])

            dve.wait_ge(S["h_st0"], 16 * ((NBLK + 1) // 2))
            dve.wait_ge(S["h_st1"], 16 * (NBLK // 2))

            with dve.Fori(0, NTB) as t:
                for c in range(C):
                    dve.wait_ge(S["h0t_hi"], C * t + c + 1)
                    low(ht_lo[:, c, :], psD[:, c, :], ht_hi[:, c, :], S["h0t_lo"])
                dve.wait_ge(S["at_hi_s"], 4 * t + 1)
                low(at_lo[:, 0, :], psX[:], at_hi[:, 0, :], S["at_lo_s"])
                dve.wait_ge(S["t0_ps"], t + 1)
                dve.wait_ge(S["xa_lo"], t)
                dve.tensor_tensor(r64[:], psT[0:R2, :], cst("group_mask", R2), ALU.mult).then_inc(S["t0_m"], 1)
                dve.wait_ge(S["t0_hi"], t + 1)
                low(r64_lo[:], r64[:], r64_hi[:], S["t0_lo"])

                def x1_sum(o):
                    dve.wait_ge(S["x_in"], 16 * (t + 1))
                    dve.wait_ge(S["x1_ps"], C * t + o + 1)
                    dve.scalar_tensor_tensor(out=tokf[:, o, :], in0=psD[:, o, :], scalar=bias[:, o:o + 1],
                                             in1=tokf[:, o, :], op0=ALU.add, op1=ALU.add).then_inc(S["x1_f"], 1)

                def x1_low(o):
                    dve.wait_ge(S["x1_hi_s"], C * t + o + 1)
                    low(x1_lo[:, o, :], tokf[:, o, :], x1_hi[:, o, :], S["x1_lo_s"])

                x1_sum(0)
                for o in range(1, C):
                    x1_sum(o)
                    x1_low(o - 1)
                x1_low(C - 1)
                for k in range(1, 4):
                    dve.wait_ge(S["at_hi_s"], 4 * t + k + 1)
                    low(at_lo[:, k % 2, :], (psX, psT)[k % 2][:], at_hi[:, k % 2, :], S["at_lo_s"])
                mask = cst("item_mask").unsqueeze(1).broadcast_to([P, NGT, GT])

                def masked(ps, s):
                    dve.tensor_tensor(tm[:].rearrange("p (g n) -> p g n", g=NGT),
                                      ps[:].rearrange("p (g n) -> p g n", g=NGT), mask, ALU.mult).then_inc(s, 1)

                dve.wait_ge(S["up_ps"], NF * t)
                for k in range(2):
                    dve.wait_ge(S["tg_ps"], 2 * t + k + 1)
                    dve.wait_ge(S["td_lo_s"], t)
                    if k:
                        dve.wait_ge(S["tg_lo_s"], 2 * t + 1)
                    masked((psG, psU)[k], S["tg_m"])
                    dve.wait_ge(S["tg_hi_s"], 2 * t + k + 1)
                    low(tg_lo[:, k, :], tm[:], tg_hi[:, k, :], S["tg_lo_s"])

                def step(fc, j, par):
                    n = NF * t + fc
                    dve.wait_ge(S["ad_hi_s"], n + 1)
                    low(ad_lo[:, par, :], psX[:, 0:NGT * P], ad_hi[:, par, :], S["ad_lo_s"])
                    dve.wait_ge(S["silu_s"], n + 1)
                    dve.wait_ge(S["up_ps"], n + 1)
                    dve.wait_ge(S["act_lo_s"], n)
                    dve.tensor_tensor(act_f[:], psU[:], silu[:], ALU.mult).then_inc(S["act_f_s"], 1)
                    dve.wait_ge(S["act_hi_s"], n + 1)
                    low(act_lo[:, par, :], act_f[:], act_hi[:, par, :], S["act_lo_s"])

                chunks(dve, step, 0, 1)

                dve.wait_ge(S["td_ps"], NF * (t + 1))
                dve.wait_ge(S["tg_lo_s"], 2 * (t + 1))
                masked(psT, S["td_m"])
                dve.wait_ge(S["td_hi_s"], t + 1)
                low(td_lo[:], tm[:], td_hi[:], S["td_lo_s"])
                for o in range(C):
                    dve.wait_ge(S["h_hi_s"], C * t + o + 1)
                    low(ht_lo[:, o, :], psD[:, o, :], ht_hi[:, o, :], S["h_lo_s"])

                links = [0]

                def link(ins):
                    links[0] += 1
                    ins.then_inc(S["soft_v"], 1)
                    dve.wait_ge(S["soft_v"], LINKS * t + links[0])

                sc = soft[:, 0]
                e = soft[:, 2]
                prob = soft[:, 3]
                dve.wait_ge(S["sc_ps"], t + 1)
                link(dve.tensor_copy(sc, psG[:, 0:SUB * NR].rearrange("p (s r) -> p s r", s=SUB)))
                link(dve.tensor_reduce(soft[:, 4, :, 0], sc, AX.X, ALU.max))
                dve.tensor_tensor(soft[:, 1], sc, soft[:, 4, :, 0:1].broadcast_to([P, SUB, NR]), ALU.subtract
                                  ).then_inc(S["sc_v"], 1)
                dve.wait_ge(S["exp_s"], t + 1)
                link(dve.tensor_reduce(soft[:, 5, :, 0], e, AX.X, ALU.add))
                link(dve.reciprocal(soft[:, 5, :, 1], soft[:, 5, :, 0]))
                link(dve.tensor_tensor(prob, e, soft[:, 5, :, 1:2].broadcast_to([P, SUB, NR]), ALU.mult))
                link(dve.tensor_reduce(soft[:, 6, :, 0], prob, AX.X, ALU.max))
                link(dve.reciprocal(soft[:, 6, :, 1], soft[:, 6, :, 0]))
                dve.tensor_tensor(soft[:, 7, :, 0], soft[:, 6, :, 0], soft[:, 6, :, 1], ALU.mult)
                link(dve.tensor_tensor(soft[:, 8], prob, soft[:, 6, :, 0:1].broadcast_to([P, SUB, NR]), ALU.is_ge))
                link(dve.tensor_scalar(soft[:, 9], soft[:, 8], -1.0, 1.0, ALU.mult, ALU.add))
                link(dve.tensor_copy(soft[:, 10, :, 0], soft[:, 7, :, 0]))
                for k in range(1, NR):
                    link(dve.tensor_tensor(soft[:, 10, :, k], soft[:, 10, :, k - 1], soft[:, 9, :, k - 1], ALU.mult))
                assert links[0] == LINKS
                lo = 0
                dve.wait_ge(S["mask_ps"], SUB * t)
                for k, hi in enumerate(RANKS):
                    last = dve.tensor_copy(mexp[:, :, lo:hi],
                                           soft[:, 10, :, k:k + 1].broadcast_to([P, SUB, hi - lo]))
                    lo = hi
                    last.then_inc(S["mexp_s"], 1)
                dve.wait_ge(S["mask_ps"], SUB * (t + 1))
                dve.wait_ge(S["r_sb"], 2 * (t + 1))
                dve.tensor_tensor(r64[:], psU[0:RMAX, :], scores[0:RMAX, :], ALU.mult).then_inc(S["xa_m"], 1)
                dve.wait_ge(S["xa_hi"], t + 1)
                low(r64_lo[:], r64[:], r64_hi[:], S["xa_lo"])
                dve.wait_ge(S["out_st"], 16 * t)
                for o in range(C):
                    dve.wait_ge(S["out_ps"], C * t + o + 1)
                    dve.scalar_tensor_tensor(out=ob[:, o, :], in0=psD[:, o, :], scalar=bias[:, C + o:C + o + 1],
                                             in1=x1_hi[:, o, :], op0=ALU.add, op1=ALU.add).then_inc(S["out_v"], 1)
                for o in range(C):
                    dve.wait_ge(S["out_v"], C * t + o + 1)
                    dve.tensor_tensor(ob[:, o, :], ob[:, o, :], x1_lo[:, o, :], ALU.add).then_inc(S["out_f"], 1)

        @block.tensor
        def _(pe):
            ident = cst("ident")

            def product(ps, w, x, start, stop):
                (wh, wl), (xh, xl) = w, x
                pe.matmul(ps, wh, xh, start=start, stop=False, skip_group_check=True)
                pe.matmul(ps, wh, xl, start=False, stop=False, skip_group_check=True)
                return pe.matmul(ps, wl, xh, start=False, stop=stop, skip_group_check=True)

            def both(hi, lo, *ix):
                return hi[ix], lo[ix]

            al = slice(None)
            pe.wait_ge(S["const_in"], 16)
            pe.wait_ge(S["ids_f"], 1)
            pe.matmul(psX[0:ITEMS, 0:N_COND], cst("before", ITEMS), onehot[:], start=True, stop=True)
            pe.matmul(psX[0:ITEMS, N_COND:2 * N_COND], cst("ones", ITEMS)[:, 0:ITEMS], onehot[:],
                      start=True, stop=True).then_inc(S["sort_ps1"], 1)
            pe.wait_ge(S["prep_lo"], 1)
            for c in range(C):
                product(psD[:, c, :], both(sh_hi, sh_lo, al, 0, slice(c * P, c * P + P)),
                        both(sh_hi, sh_lo, al, 1, al), True, True).then_inc(S["kern_ps"], 1)
            pe.wait_ge(S["sort_v"], 11)
            pe.matmul(psX[:, 0:SLOTS], cst("item_no", ITEMS), perm[:], start=True, stop=True)
            pe.matmul(psX[:, SLOTS:2 * SLOTS], cst("ones", ITEMS), perm[:], start=True, stop=True)
            pe.matmul(psX[0:1, 2 * SLOTS:3 * SLOTS], ids0f[:], perm[:], start=True, stop=True
                      ).then_inc(S["sort_ps2"], 1)
            pe.wait_ge(S["prep_lo"], 3)
            for c in range(C):
                ps = (psG, psU)[c // 2][:, (c % 2) * 256:(c % 2) * 256 + 256]
                for k in range(4):
                    mm = product(ps, both(lora_hi, lora_lo, al, 0, k, slice(c * P, c * P + P)),
                                 both(g_hi, g_lo, al, k, al), k == 0, k == 3)
                if c % 2:
                    mm.then_inc(S["aeff_ps"], 1)
            for j in range(NTB):
                pe.wait_ge(S["kern_f"], C)
                for k in range(4):
                    mm = product(psD[0:R2, j, :], both(g_hi, g_lo, al, k, slice(j * R2, (j + 1) * R2)),
                                 both(lora_hi, lora_lo, al, 1, k, al), k == 0, k == 3)
                mm.then_inc(S["beff_ps"], 1)

            def turn(par, it):
                pe.wait_ge(S[f"xs_in{par}"], 16 * it + 16)
                pe.wait_ge(S[f"xs_lo{par}"], it)
                for c in range(C):
                    mm = pe.transpose((psG, psU)[par][:, c * P:c * P + P], xs[:, par, c * P:c * P + P], ident)
                mm.then_inc(S[f"xs_ps{par}"], 1)

            def cond(par, b, it):
                e = pe.value_load(blk_adp[0:1, bass.ds(b * BI, 1)], min_val=0, max_val=N_COND - 1)
                pe.wait_ge(S[f"xs_hi{par}"], it + 1)
                pe.wait_ge(S[f"xs_lo{par}"], it + 1)
                pe.wait_ge(S[f"h_out{par}"], it)
                ps = (psT, psX)[par][:]
                for c in range(C):
                    w = [v[:, bass.ds(e, 1), c * D:(c + 1) * D].rearrange("p e n -> p (e n)") for v in (w_hi, w_lo)]
                    xh, xl = xs_hi[:, par, c * P:c * P + P], xs_lo[:, par, c * P:c * P + P]
                    pe.matmul(ps, xh, w[0], start=c == 0, stop=False)
                    pe.matmul(ps, xl, w[0], start=False, stop=False)
                    mm = pe.matmul(ps, xh, w[1], start=False, stop=c == C - 1)
                mm.then_inc(S[f"h_ps{par}"], 1)

            pe.wait_ge(S["aeff_done"], 2)
            pe.wait_ge(S["idx_ready"], 1)
            turn(0, 0)
            turn(1, 0)
            for h in range(2):
                pe.wait_ge(S[f"w_lo_s{h}"], N_COND)
            with pe.Fori(0, NBLK // 2 - 1) as it:
                cond(0, 2 * it, it)
                turn(0, it + 1)
                cond(1, 2 * it + 1, it)
                turn(1, it + 1)
            cond(0, NBLK - 2, NBLK // 2 - 1)
            cond(1, NBLK - 1, NBLK // 2 - 1)
            for par in range(2):
                pe.wait_ge(S[f"h_out{par}"], NBLK // 2)

            with pe.Fori(0, NTB) as t:
                pe.wait_ge(S["h0_in"], 16 * t + 16)
                for c in range(C):
                    pe.wait_ge(S["out_v"], C * t)
                    for s in range(SUB):
                        mm = pe.transpose(psD[:, c, s * P:s * P + P], tok[:, s, c * P:c * P + P], ident)
                    mm.then_inc(S["h0t_ps"], 1)

                def turn_a(k):
                    ps = (psX, psT)[k % 2]
                    for c in range(C):
                        at = (k // 2) * D + c * P
                        mm = pe.transpose(ps[:, c * P:c * P + P], fix[:, k % 2, at:at + P], ident)
                    mm.then_inc(S["at_ps"], 1)

                pe.wait_ge(S["fix_in"], 16 * NGT * (t + 1))
                pe.wait_ge(S["r_sb"], 2 * t)
                turn_a(0)
                pe.wait_ge(S["ae_l"], t + 1)
                pe.wait_ge(S["td_m"], t)
                for c in range(C):
                    pe.wait_ge(S["h0t_lo"], C * t + c + 1)
                    mm = product(psT[0:R2, :], both(ae_hi, ae_lo, al, c, al), both(ht_hi, ht_lo, al, c, al),
                                 c == 0, c == C - 1)
                mm.then_inc(S["t0_ps"], 1)
                for o in range(C):
                    for c in range(C):
                        product(psD[:, o, :], both(k_hi, k_lo, al, c, slice(o * P, o * P + P)),
                                both(ht_hi, ht_lo, al, c, al), c == 0, False)
                pe.wait_ge(S["be_l"], t + 1)
                pe.wait_ge(S["t0_lo"], t + 1)
                for o in range(C):
                    product(psD[:, o, :], both(be_hi, be_lo, al, slice(o * P, o * P + P)),
                            (r64_hi[:], r64_lo[:]), False, True).then_inc(S["x1_ps"], 1)
                turn_a(1)

                def ranks(k):
                    pe.wait_ge(S["at_lo_s"], 4 * t + k + 1)
                    g = k % 2
                    ps = (psG, psU)[k // 2][:, g * GT:g * GT + GT]
                    for c in range(C):
                        if k == 0:
                            pe.wait_ge(S["x1_lo_s"], C * t + c + 1)
                        mm = product(ps, both(at_hi, at_lo, al, k % 2, slice(c * P, c * P + P)),
                                     both(x1_hi, x1_lo, al, c, slice(g * GT, g * GT + GT)), c == 0, c == C - 1)
                    if g:
                        mm.then_inc(S["tg_ps"], 1)

                pe.wait_ge(S["mexp_s"], NR * t)
                ranks(0)
                turn_a(2)
                ranks(1)
                turn_a(3)
                ranks(2)
                ranks(3)

                def down(par, n, opens, closes):
                    pe.wait_ge(S["act_hi_s"], n)
                    pe.wait_ge(S["act_lo_s"], n)
                    pe.wait_ge(S["ad_lo_s"], n)
                    for g in range(NGT):
                        cols = slice(g * GT, g * GT + GT)
                        mm = product(psT[:, cols], both(ad_hi, ad_lo, al, par, slice(g * P, g * P + P)),
                                     both(act_hi, act_lo, al, par, cols), opens and g == 0, closes)
                    mm.then_inc(S["td_ps"], 1)
                    pe.wait_ge(S["dn_lo_s"], n)
                    for o in range(C):
                        mm = product(psD[:, o, :], both(dn_hi, dn_lo, al, par, slice(o * P, o * P + P)),
                                     both(act_hi, act_lo, al, par, al), opens, False)
                    mm.then_inc(S["dn_ps"], 1)

                def step(fc, j, par):
                    n = NF * t + fc
                    first = isinstance(fc, int) and fc == 0
                    pe.wait_ge(S["bu_hi_s"], n + 1)
                    pe.wait_ge(S["ad_lo_s"], n)
                    if first:
                        pe.wait_ge(S["at_lo_s"], 4 * t + 4)
                    for g in range(NGT):
                        mm = pe.transpose(psX[:, g * P:g * P + P], ab[:, par, g, 0:P], ident)
                    mm.then_inc(S["ad_ps"], 1)
                    pe.wait_ge(S["gu_lo_s"], n + 1)
                    pe.wait_ge(S["silu_s"], n)
                    pe.wait_ge(S["act_f_s"], n)
                    if first:
                        pe.wait_ge(S["tg_m"], 2 * t + 2)
                    for k, ps in enumerate((psG, psU)):
                        for c in range(C):
                            at = k * D + c * P
                            product(ps[:], both(gu_hi, gu_lo, al, par, slice(at, at + P)),
                                    both(x1_hi, x1_lo, al, c, al), c == 0, False)
                    if first:
                        pe.wait_ge(S["tg_lo_s"], 2 * t + 2)
                    pe.wait_ge(S["bu_lo_s"], n + 1)
                    for k, (ps, s) in enumerate(((psG, "gate_ps"), (psU, "up_ps"))):
                        for g in range(NGT):
                            cols = slice(g * GT, g * GT + GT)
                            mm = product(ps[:, cols], both(bu_hi, bu_lo, al, par, g, slice(k * P, k * P + P)),
                                         both(tg_hi, tg_lo, al, k, cols), False, True)
                        mm.then_inc(S[s], 1)
                    if not first:
                        down(1 - par, n, isinstance(fc, int) and fc == 1, False)

                chunks(pe, step, 2, 1)
                down((NF - 1) % 2, NF * (t + 1), False, True)

                pe.wait_ge(S["td_hi_s"], t + 1)
                pe.wait_ge(S["td_lo_s"], t + 1)
                pe.wait_ge(S["bd_lo_s"], t + 1)
                for o in range(C):
                    for g in range(NGT):
                        cols = slice(g * GT, g * GT + GT)
                        mm = product(psD[:, o, cols], both(bd_hi, bd_lo, al, g, slice(o * P, o * P + P)),
                                     both(td_hi, td_lo, al, cols), False, True)
                    mm.then_inc(S["h_ps"], 1)
                pe.wait_ge(S["wf_lo_s"], 3)
                for c in range(C):
                    pe.wait_ge(S["h_lo_s"], C * t + c + 1)
                    mm = product(psX[0:RS, :], both(ra_hi, ra_lo, al, c, al), both(ht_hi, ht_lo, al, c, al),
                                 c == 0, c == C - 1)
                mm.then_inc(S["r_ps"], 1)

                def linear(o):
                    for c in range(C):
                        product(psD[:, o, :], both(wf_hi, wf_lo, al, c, slice(o * P, o * P + P)),
                                both(ht_hi, ht_lo, al, c, al), c == 0, False)

                linear(0)
                count0 = value(pe, 2 * t + 1)
                alone(pe)
                pe.wait_ge(S["r_sb"], count0)
                for s in range(SUB):
                    mm = pe.transpose(psG[:, s * NR:(s + 1) * NR], scores[RMAX:RS, s * P:(s + 1) * P],
                                      const[RMAX:RS, RMAX:RS])
                mm.then_inc(S["sc_ps"], 1)
                linear(1)
                linear(2)
                count0 = value(pe, NR * (t + 1))
                alone(pe)
                pe.wait_ge(S["mexp_s"], count0)
                for s in range(SUB):
                    pe.transpose(psU[0:RMAX, s * P:(s + 1) * P], mexp[:, s, :], ident).then_inc(S["mask_ps"], 1)
                linear(3)
                pe.wait_ge(S["xa_lo"], t + 1)
                for o in range(C):
                    product(psD[:, o, :], both(rb_hi, rb_lo, al, slice(o * P, o * P + P)),
                            (r64_hi[:], r64_lo[:]), False, True).then_inc(S["out_ps"], 1)


def kernel(**inputs):
    import concourse.bacc as bacc
    from concourse.bass_utils import run_bass_kernel_spmd as run

    v = {k: np.asarray(x) for k, x in inputs.items()}

    def features(w):
        *rest, f, n = w.shape
        return np.moveaxis(w.reshape(*rest, f // P, P, n), -3, -2)

    def padded(w, axis):
        width = [(0, 0)] * w.ndim
        width[axis] = (0, NF * P - F)
        return np.pad(w, width)

    x = v["x"].reshape(TOKENS, D)
    bias = np.zeros((P, 2 * C + 1), np.float32)
    bias[:, 0:C] = v["L0_ffn_bias"].reshape(C, P).T
    bias[:, C:2 * C] = v["L1_ffn_b"].reshape(C, P).T
    bias[RMAX:RMAX + NR, 2 * C] = v["L1_ffn_gate_b"]
    gate = v["L0_ffn_gate"].reshape(GROUPS, 4, N_LORA // 4)
    gu = np.stack([padded(v["L1_cond_W_gate"], 0), padded(v["L1_cond_W_up"], 0)])
    gu = gu.reshape(2, NF, P, C, P).transpose(1, 4, 0, 3, 2)
    dn = padded(v["L1_cond_W_down"], 1).reshape(D, NF, P).transpose(1, 2, 0)
    ab = np.stack([
        padded(v["L1_cond_A_down"][0], 2),
        padded(v["L1_cond_B_gate"][0], 1).transpose(0, 2, 1),
        padded(v["L1_cond_B_up"][0], 1).transpose(0, 2, 1),
    ]).reshape(3, N_ADP * RANK1, NF, P).transpose(2, 1, 0, 3)
    fix = np.stack([v["L1_cond_A_gate"][0], v["L1_cond_A_up"][0], v["L1_cond_B_down"][0].transpose(0, 2, 1)], 2)
    arrays = {
        "x": x,
        "x_t": x.reshape(NTB, TB, C, P).transpose(0, 3, 2, 1).reshape(NTB, P, C * TB),
        "const": constants(),
        "ids0": v["itok_B_3_7"].reshape(ITEMS, 1),
        "ids1": np.repeat(v["itok_B_2_6"].reshape(ITEMS // GI, GI), RANK1, 1).T,
        "gate": np.repeat(gate.transpose(2, 1, 0), RANK0, 0),
        "bias": bias,
        "shared": np.stack([v["L0_ffn_lora_A_shared"], v["L0_ffn_lora_B_shared"].T], 1),
        "lora": np.stack([v["L0_ffn_lora_A"].reshape(4, P, D),
                          v["L0_ffn_lora_B"].transpose(0, 2, 1).reshape(4, P, D)]).transpose(2, 0, 1, 3),
        "kern": features(v["L0_ffn_kernel"]),
        "cond_w": features(v["L0_cond_weight"].transpose(0, 2, 1)).reshape(N_COND, P, C * D),
        "wf": features(v["L1_ffn_W"].T),
        "ra": features(np.concatenate([v["L1_ffn_A"].T, v["L1_ffn_gate_w"].T], 1)),
        "rb": v["L1_ffn_B"].T,
        "gu": gu.reshape(NF, P, 2 * D),
        "dn": dn,
        "ab": ab.reshape(NF * N_ADP * RANK1, STAB),
        "fix": fix.reshape(N_ADP * RANK1, FIX),
    }
    arrays = {"in_" + k: np.ascontiguousarray(w) for k, w in arrays.items()}
    nc = bacc.Bacc("TRN2", target_bir_lowering=False, num_devices=1)
    drams = {k[3:]: nc.dram_tensor(k, w.shape, mybir.dt.from_np(w.dtype), kind="ExternalInput").ap()
             for k, w in arrays.items()}
    out = nc.dram_tensor("out_t", (NTB, P, C * TB), F32, kind="ExternalOutput").ap()
    two_layers(nc, drams, out)
    got = run(nc, [arrays], core_ids=[0]).results[0]["out_t"]
    return got.reshape(NTB, P, C, TB).transpose(0, 3, 2, 1).reshape(ITEMS, ITEM_T, D)
```

```python
from contextlib import ExitStack

import numpy as np

import concourse.bass as bass
from concourse import mybir

F32 = mybir.dt.float32
F32R = mybir.dt.float32r
I32 = mybir.dt.int32
U32 = mybir.dt.uint32
ACT = mybir.ActivationFunctionType
ALU = mybir.AluOpType
AX = mybir.AxisListType

P = 128
ITEMS, ITEM_T, D = 64, 32, 512
TOKENS = ITEMS * ITEM_T
C = D // P
N_COND = 8
GROUPS, N_LORA, RANK0 = 8, 16, 32
BI = 4
BT = BI * ITEM_T
NBLK = (ITEMS + N_COND * (BI - 1)) // BI
SLOTS = NBLK * BI
F = 1376
NF = -(-F // P)
N_ADP, RANK1 = 16, 16
GI = P // RANK1
GT = GI * ITEM_T
RANKS = (8, 16, 32, 64)
RMAX = RANKS[-1]
NR = len(RANKS)
RS = RMAX + NR
LINKS = 9 + NR
TB = 512
NTB = TOKENS // TB
NGT = TB // GT
SUB = TB // P
UNROLL = 4
RING = 4
PREP_AT = 6
GPB = TB * GROUPS // TOKENS
R2 = GPB * RANK0
STAB = 3 * P
FIX = 3 * D

CONST_W = {
    "ident": P, "item_mask": GT, "group_mask": TB, "delta": RANK0, "ones": P, "before": ITEMS,
    "item_no": P, "adapter_no": N_COND, "fours": ITEMS // BI, "earlier": N_COND * N_COND, "slot_no": SLOTS,
    "dummy": SLOTS, "quadrant": BI, "row_in_item": 1, "chunk_row": NF + 1, "rank_row": 1,
}
CONST_AT = {}
_at = 0
for _k, _w in CONST_W.items():
    CONST_AT[_k] = _at
    _at += _w
CONST_N = _at


def constants():
    c = np.zeros((P, CONST_N), np.float32)

    def put(name, a):
        a = np.asarray(a, np.float32)
        a = a.reshape(a.shape[0], -1)
        c[:a.shape[0], CONST_AT[name]:CONST_AT[name] + a.shape[1]] = a

    p = np.arange(P)[:, None]
    put("ident", np.eye(P))
    put("item_mask", 0.5 * (p // RANK1 == np.arange(GT)[None] // ITEM_T))
    put("group_mask", p // RANK0 == np.arange(TB)[None] // (TOKENS // GROUPS))
    put("delta", p % RANK0 == np.arange(RANK0)[None])
    put("ones", np.ones((P, P)))
    put("before", np.arange(ITEMS)[:, None] < np.arange(ITEMS)[None])
    put("item_no", np.broadcast_to(np.arange(ITEMS)[:, None], (ITEMS, P)))
    put("adapter_no", np.broadcast_to(np.arange(N_COND), (P, N_COND)))
    put("fours", np.broadcast_to(BI * np.arange(ITEMS // BI), (P, ITEMS // BI)))
    e = np.arange(N_COND)
    put("earlier", np.broadcast_to((e[None] < e[:, None]).reshape(1, -1), (P, N_COND ** 2)))
    put("slot_no", np.broadcast_to(np.arange(SLOTS), (P, SLOTS)))
    put("dummy", np.broadcast_to(ITEMS + np.arange(SLOTS), (P, SLOTS)))
    put("quadrant", p // ITEM_T == np.arange(BI)[None])
    put("row_in_item", p % ITEM_T)
    put("chunk_row", np.broadcast_to(np.append(np.arange(NF) * N_ADP * RANK1, 0), (P, NF + 1)))
    put("rank_row", p % RANK1)
    return c


def two_layers(nc, a, out):
    with ExitStack() as ctx:
        base = -(-nc.sbuf_base // 64) * 64
        top = {"at": base}

        def sb(name, shape, dt, at=None):
            size = 4 * int(np.prod(shape[1:]))
            if at is None:
                at = top["at"]
                top["at"] = at + -(-size // 32) * 32
            return nc.alloc_sbuf_tensor_at(name, list(shape), dt, offset=at)

        def pair(name, shape):
            return sb(name + "_hi", shape, F32R), sb(name + "_lo", shape, F32R)

        def psum(name, shape):
            return ctx.enter_context(nc.psum_tensor(name, list(shape), F32))

        def sem(name):
            return ctx.enter_context(nc.semaphore(name))

        const = sb("const", [P, CONST_N], F32)
        bias = sb("bias", [P, 2 * C + 1], F32)
        k_hi, k_lo = pair("kern", [P, C, D])
        a_eff = sb("a_eff", [P, C, GROUPS * RANK0], F32)
        b_eff_at = top["at"]
        b_eff = sb("b_eff", [R2, NTB, D], F32)
        wf_at = top["at"]
        wf_raw = sb("wf_raw", [P, C, D], F32)
        wf_lo = sb("wf_lo", [P, C, D], F32R, at=wf_at)
        ra_at = top["at"]
        ra_raw = sb("ra_raw", [P, C, RS], F32)
        ra_lo = sb("ra_lo", [P, C, RS], F32R, at=ra_at)
        rb_at = top["at"]
        rb_raw = sb("rb_raw", [RMAX, D], F32)
        rb_lo = sb("rb_lo", [RMAX, D], F32R, at=rb_at)
        idx_tab = sb("idx_tab", [P, ITEMS // GI, NF + 1], U32)
        shared_from = top["at"]

        w_hi = sb("cond_w_hi", [P, N_COND, C * D], F32R)
        w_at = top["at"]
        w_raw = sb("cond_w_raw", [P, N_COND, C * D], F32)
        w_lo = sb("cond_w_lo", [P, N_COND, C * D], F32R, at=w_at)
        xs_at = top["at"]
        xs = sb("xs", [P, RING, D], F32)
        xt_at = top["at"]
        xs_hi, xs_lo = pair("xs_t", [P, 2, D])
        h0 = sb("h0", [P, 2, D], F32)
        kraw_at = top["at"]
        kraw = sb("kraw", [P, C, D], F32)
        small_at = top["at"]
        top["at"] = shared_from + PREP_AT * 4 * C * D
        lora_at = top["at"]
        lora_a = sb("lora_a", [P, 4, D], F32)
        la_lo = sb("lora_a_lo", [P, 4, D], F32R, at=lora_at)
        la_hi = sb("lora_a_hi", [P, 4, D], F32R)
        assert top["at"] <= shared_from + N_COND * 4 * C * D
        lora_b = sb("lora_b", [P, 4, D], F32, at=kraw_at)
        lb_lo = sb("lora_b_lo", [P, 4, D], F32R, at=kraw_at)
        lb_hi = sb("lora_b_hi", [P, 4, D], F32R, at=xs_at)
        assert RING * D >= 4 * D
        sh = sb("shared", [RANK0, 2, D], F32, at=xt_at)
        sh_lo = sb("shared_lo", [RANK0, 2, D], F32R, at=xt_at)
        sh_hi = sb("shared_hi", [RANK0, 2, D], F32R, at=xt_at + 4 * 2 * D)
        gsel = sb("gsel", [P, 4, GROUPS * RANK0], F32, at=b_eff_at)
        g_lo = sb("gsel_lo", [P, 4, GROUPS * RANK0], F32R, at=b_eff_at)
        g_hi = sb("gsel_hi", [P, 4, GROUPS * RANK0], F32R, at=b_eff_at + 4 * 4 * GROUPS * RANK0)
        assert 2 * 4 * GROUPS * RANK0 <= NTB * D
        top["at"] = small_at
        gate_v = sb("gate_v", [P, 4, GROUPS], F32)
        ids0 = sb("ids0", [ITEMS, 1], I32)
        ids0f = sb("ids0f", [ITEMS, 1], F32)
        ids1 = sb("ids1", [P, GROUPS], I32)
        ids1f = sb("ids1f", [P, GROUPS], F32)
        onehot = sb("onehot", [ITEMS, N_COND], F32)
        over = sb("over", [ITEMS, N_COND, ITEMS // BI], F32)
        nblk = sb("nblk", [ITEMS, N_COND], F32)
        earlier = sb("earlier_n", [ITEMS, N_COND, N_COND], F32)
        start = sb("start", [ITEMS, N_COND], F32)
        place = sb("place", [ITEMS, N_COND], F32)
        own = sb("own", [ITEMS, N_COND], F32)
        slot = sb("slot", [ITEMS, 1], F32)
        perm = sb("perm", [ITEMS, SLOTS], F32)
        item_g = sb("item_g", [P, SLOTS], F32)
        empty = sb("empty", [P, SLOTS], F32)
        dummy = sb("dummy_s", [P, SLOTS], F32)
        item_s = sb("item_s", [P, SLOTS], F32)
        sel_g = sb("sel_g", [P, NBLK, BI], F32)
        sel_s = sb("sel_s", [P, NBLK, BI], F32)
        row_g = sb("row_g", [P, NBLK], F32)
        row_s = sb("row_s", [P, NBLK], F32)
        idx_base = sb("idx_base", [P, GROUPS], F32)
        idx_g = sb("idx_g", [P, NBLK], U32)
        idx_s = sb("idx_s", [P, NBLK], U32)
        idx_gn = sb("idx_gn", [P, RING], U32)
        idx_sn = sb("idx_sn", [P, 2], U32)
        blk_adp = sb("blk_adp", [1, SLOTS], I32)
        cond_top = top["at"]
        assert cond_top <= nc.sbuf_usable_end

        top["at"] = shared_from
        wf_hi = sb("wf_hi", [P, C, D], F32R)
        ra_hi = sb("ra_hi", [P, C, RS], F32R)
        rb_hi = sb("rb_hi", [RMAX, D], F32R)
        tok_at = top["at"]
        tok = sb("tok", [P, SUB, D], F32)
        tokf = sb("x_t", [P, C, TB], F32, at=tok_at)
        ht_hi, ht_lo = pair("ht", [P, C, TB])
        x1_hi, x1_lo = pair("x1", [P, C, TB])
        ae_hi, ae_lo = pair("ae", [P, C, R2])
        r64_hi, r64_lo = pair("r64", [RMAX, TB])
        fix = sb("fix", [P, NGT, FIX], F32)
        at_hi, at_lo = pair("at", [P, 2, D])
        tm = sb("tm", [P, TB], F32)
        tg_at = top["at"]
        tg_hi, tg_lo = pair("tg", [P, 2, TB])
        be_at = top["at"]
        td_hi, td_lo = pair("td", [P, TB])
        be_hi = sb("be_hi", [R2, D], F32R, at=be_at)
        be_lo = sb("be_lo", [R2, D], F32R, at=be_at + 4 * TB)
        bd_hi, bd_lo = pair("bd", [P, NGT, D])
        gu_raw = sb("gu_raw", [P, 2 * D], F32)
        gu_hi, gu_lo = pair("gu", [P, 2, 2 * D])
        dn_raw = sb("dn_raw", [P, D], F32)
        dn_hi, dn_lo = pair("dn", [P, 2, D])
        ab = sb("ab", [P, 2, NGT, STAB], F32)
        bu_hi, bu_lo = pair("bu", [P, 2, NGT, 2 * P])
        ad_hi, ad_lo = pair("ad", [P, 2, NGT * P])
        scores_at = top["at"]
        silu = sb("silu", [P, TB], F32)
        r64_at = top["at"]
        act_f = sb("act_f", [P, TB], F32)
        act_hi, act_lo = pair("act", [P, 2, TB])
        idx_blk = sb("idx_blk", [P, NGT, NF + 1], U32)
        idx_row = sb("idx_row", [P, 2, NGT], U32)
        scores = sb("scores", [RS, TB], F32, at=scores_at)
        r64 = sb("r64", [RMAX, TB], F32, at=r64_at)
        soft = sb("soft", [P, 12, SUB, NR], F32)
        mexp = sb("mexp", [P, SUB, RMAX], F32)
        main_top = top["at"]
        assert main_top <= nc.sbuf_usable_end
        ob = sb("out_b", [P, C, TB], F32, at=tg_at)

        psD = psum("psD", [P, 4, TB])
        psT = psum("psT", [P, TB])
        psG = psum("psG", [P, TB])
        psU = psum("psU", [P, TB])
        psX = psum("psX", [P, TB])
        H0_BANK = (psX, psT, psG, psU)
        A_BANK = (psT, psG, psT, psX)

        def cst(name, rows=P):
            return const[0:rows, CONST_AT[name]:CONST_AT[name] + CONST_W[name]]

        h0_dram = nc.dram_tensor("h0_scratch", [TOKENS + SLOTS * ITEM_T, D], F32, kind="Internal").ap()

        names = """const_in small_in lora_in kraw_in late_in w_in0 w_in1
            ids_f sort_v sort_ps1 sort_ps2 idx_ready idx_tab_ready
            gsel_f prep_hi lora_hi_s lora_lo_s lora_b_in lb_hi_s lb_lo_s sh_lo_s g_lo_s kern_ps kern_f kern_hi kern_lo aeff_ps beff_ps aeff_done beff_done
            w_hi_s w_lo_s xs_in0 xs_in1 xs_in2 xs_in3 xs_ps0 xs_ps1 xs_ps2 xs_ps3 xs_hi0 xs_hi1 xs_lo0 xs_lo1 h_ps0 h_ps1 h_out0 h_out1
            h_st0 h_st1
            wf_hi_s wf_lo_s
            h0_in h0t_ps h0t_hi h0t_lo ae_s be_s ae_l be_l x_in t0_ps t0_m t0_hi t0_lo x1_ps x1_f x1_hi_s x1_lo_s
            idx_b fix_in at_ps at_hi_s at_lo_s tg_ps tg_m tg_hi_s tg_lo_s bd_hi_s bd_lo_s
            idx_r idx_gn0 idx_gn1 idx_gn2 idx_gn3 idx_sn0 idx_sn1 gu_in dn_in ab_in0 ab_in1 gu_hi_s gu_lo_s bu_hi_s bu_lo_s dn_hi_s dn_lo_s
            ad_ps ad_hi_s ad_lo_s gate_ps up_ps silu_s act_f_s act_hi_s act_lo_s td_ps dn_ps
            td_m td_hi_s td_lo_s h_ps h_hi_s h_lo_s r_ps r_sb sc_ps sc_v exp_s soft_v mexp_s mask_ps
            xa_m xa_hi xa_lo lin_ps out_ps out_v out_f out_st""".split()
        S = {n: sem(n) for n in names}

        block = ctx.enter_context(nc.Block())

        def value(eng, count):
            return count if isinstance(count, int) else eng.to_reg(count)

        def alone(eng):
            eng.wait_ge(S["const_in"], 16)

        def last(fc, before=0):
            return isinstance(fc, int) and fc == NF - 1 - before

        def chunks(eng, body, head, tail):
            rounds = (NF - head - tail) // UNROLL
            for fc in range(head):
                body(fc, fc // 2, fc % 2)
            with eng.Fori(0, rounds) as i:
                for k in range(head, head + UNROLL):
                    body(UNROLL * i + k, UNROLL // 2 * i + k // 2, k % 2)
            for fc in range(head + UNROLL * rounds, NF):
                body(fc, fc // 2, fc % 2)

        def blocks(eng, body, head=0):
            rounds = (NBLK - head) // RING
            with eng.Fori(0, rounds) as i:
                for k in range(head, head + RING):
                    body(RING * i + k, k % RING, i + k // RING, 2 * i + k // 2)
            for b in range(head + RING * rounds, NBLK):
                body(b, b % RING, b // RING, b // 2)

        def multiplied(eng):
            for par in range(2):
                eng.wait_ge(S[f"h_ps{par}"], NBLK // 2)

        def scattered(eng):
            for par in range(2):
                eng.wait_ge(S[f"h_st{par}"], 16 * (NBLK // 2))

        def token_blocks(eng, body):
            with eng.Fori(0, NTB - 1) as t:
                body(t, True)
            body(NTB - 1, False)

        @block.sync
        def _(sp):
            sp.dma_start(ids0[:], a["ids0"]).then_inc(S["small_in"], 16)
            sp.dma_start(ids1[:], a["ids1"]).then_inc(S["small_in"], 16)
            sp.dma_start(const[:], a["const"]).then_inc(S["const_in"], 16)
            sp.dma_start(gate_v[:], a["gate"]).then_inc(S["small_in"], 16)
            sp.dma_start(bias[:], a["bias"]).then_inc(S["small_in"], 16)
            sp.dma_start(sh[:], a["shared"]).then_inc(S["small_in"], 16)
            sp.dma_start(lora_a[:], a["lora_a"]).then_inc(S["lora_in"], 16)
            sp.dma_start(kraw[:], a["kern"]).then_inc(S["kraw_in"], 16)
            for e in range(N_COND):
                sp.dma_start(w_raw[:, e, :], a["cond_w"][e]).then_inc(S[f"w_in{e % 2}"], 16)
                if e:
                    sp.wait_ge(S[f"w_in{(e - 1) % 2}"], 16 * ((e + 1) // 2))
            sp.dma_start(wf_raw[:], a["wf"]).then_inc(S["late_in"], 16)
            sp.dma_start(ra_raw[:], a["ra"]).then_inc(S["late_in"], 16)
            sp.dma_start(rb_raw[:], a["rb"]).then_inc(S["late_in"], 16)
            sp.wait_ge(S["kern_lo"], 1)
            sp.dma_start(lora_b[:], a["lora_b"]).then_inc(S["lora_b_in"], 16)
            scattered(sp)
            h0_rows = h0_dram[0:TOKENS, :].rearrange("(t s p) d -> t p s d", s=SUB, p=P)

            def load_h0(t):
                sp.wait_ge(S["x1_hi_s"], C * t)
                sp.wait_ge(S["x1_lo_s"], C * t)
                sp.dma_start(tok[:], h0_rows[bass.ds(t, 1)].rearrange("t p s d -> (t p) s d")
                             ).then_inc(S["h0_in"], 16)

            load_h0(0)

            def body(t, more):
                sp.wait_ge(S["h0t_ps"], C * t + C)
                sp.dma_start(tokf[:], a["x_t"][bass.ds(t, 1), :, :].rearrange("t p (c n) -> (t p) c n", c=C)
                             ).then_inc(S["x_in"], 16)

                def load(fc, j, par):
                    n = NF * t + fc
                    sp.wait_ge(S["gu_hi_s"], n)
                    sp.wait_ge(S["gu_lo_s"], n)
                    sp.dma_start(gu_raw[:], a["gu"][bass.ds(fc, 1), :, :].rearrange("f p n -> (f p) n")
                                 ).then_inc(S["gu_in"], 16)
                    sp.wait_ge(S["dn_hi_s"], n)
                    sp.wait_ge(S["dn_lo_s"], n)
                    sp.dma_start(dn_raw[:], a["dn"][bass.ds(fc, 1), :, :].rearrange("f p n -> (f p) n")
                                 ).then_inc(S["dn_in"], 16)

                chunks(sp, load, 0, 1)
                if more:
                    load_h0(t + 1)

            token_blocks(sp, body)

        @block.gpsimd
        def _(pool):
            def low(dst, x, hi, s):
                pool.tensor_tensor(dst, x, hi, ALU.subtract).then_inc(s, 1)

            pool.wait_ge(S["const_in"], 16)
            pool.wait_ge(S["small_in"], 80)
            pool.tensor_tensor(gsel[:].rearrange("p k (g r) -> p (k g) r", r=RANK0),
                               cst("delta").unsqueeze(1).broadcast_to([P, 4 * GROUPS, RANK0]),
                               gate_v[:].rearrange("p k g -> p (k g)").unsqueeze(2).broadcast_to([P, 4 * GROUPS, RANK0]),
                               ALU.mult).then_inc(S["gsel_f"], 1)
            pool.wait_ge(S["prep_hi"], 1)
            low(sh_lo[:], sh[:], sh_hi[:], S["sh_lo_s"])
            pool.wait_ge(S["prep_hi"], 2)
            low(g_lo[:], gsel[:], g_hi[:], S["g_lo_s"])

            def gather(b, ring, i, j):
                count = value(pool, i)
                alone(pool)
                pool.wait_ge(S[f"xs_ps{ring}"], count)
                pool.tensor_copy(idx_gn[:, ring:ring + 1], idx_g[:, bass.ds(b, 1)]).then_inc(S[f"idx_gn{ring}"], 1)
                count = value(pool, i + 1)
                alone(pool)
                pool.wait_ge(S[f"idx_gn{ring}"], count)
                pool.indirect_dma_start(xs[:, ring, :], None, a["x"],
                                        bass.IndirectOffsetOnAxis(idx_gn[:, ring:ring + 1], 0)
                                        ).then_inc(S[f"xs_in{ring}"], 16)

            def scatter(b, ring, i, j):
                par = ring % 2
                count = value(pool, j + 1)
                alone(pool)
                pool.wait_ge(S[f"h_out{par}"], count)
                pool.tensor_copy(idx_sn[:, par:par + 1], idx_s[:, bass.ds(b, 1)]).then_inc(S[f"idx_sn{par}"], 1)
                alone(pool)
                pool.wait_ge(S[f"idx_sn{par}"], count)
                pool.indirect_dma_start(h0_dram, bass.IndirectOffsetOnAxis(idx_sn[:, par:par + 1], 0),
                                        h0[:, par, :], None).then_inc(S[f"h_st{par}"], 16)

            pool.wait_ge(S["idx_ready"], 1)
            for b in range(RING):
                gather(b, b, 0, 0)
            pool.wait_ge(S["kern_hi"], 1)
            low(k_lo[:], kraw[:], k_hi[:], S["kern_lo"])

            def move(b, ring, i, j):
                scatter(b - RING, ring, i - 1, j - RING // 2)
                gather(b, ring, i, j)

            blocks(pool, move, RING)
            for b in range(NBLK - RING, NBLK):
                scatter(b, b % RING, b // RING, b // 2)

            pool.wait_ge(S["ae_s"], 1)
            low(ae_lo[:], a_eff[:, :, 0:R2], ae_hi[:], S["ae_l"])
            multiplied(pool)
            pool.wait_ge(S["idx_tab_ready"], 1)

            def rows(fc, par, n):
                pool.tensor_copy(idx_row[:, par, :].unsqueeze(2), idx_blk[:, :, bass.ds(fc, 1)]
                                 ).then_inc(S["idx_r"], 1)
                count = value(pool, n + 1)
                alone(pool)
                pool.wait_ge(S["idx_r"], count)
                for g in range(NGT):
                    pool.indirect_dma_start(ab[:, par, g, :], None, a["ab"],
                                            bass.IndirectOffsetOnAxis(idx_row[:, par, g:g + 1], 0)
                                            ).then_inc(S[f"ab_in{par}"], 16)

            def open_block(t):
                even, odd, fixed = (value(pool, 16 * NGT * k * t) for k in (NF // 2 + 1, NF // 2, 1))
                alone(pool)
                pool.wait_ge(S["ab_in0"], even)
                pool.wait_ge(S["ab_in1"], odd)
                pool.wait_ge(S["fix_in"], fixed)
                pool.tensor_copy(idx_blk[:], idx_tab[:, bass.ds(t * NGT, NGT), :]).then_inc(S["idx_b"], 1)
                copied, turned, split = value(pool, t + 1), value(pool, 4 * t), value(pool, t)
                alone(pool)
                pool.wait_ge(S["idx_b"], copied)
                pool.wait_ge(S["at_ps"], turned)
                pool.wait_ge(S["bd_hi_s"], split)
                pool.wait_ge(S["bd_lo_s"], split)
                for g in range(NGT):
                    pool.indirect_dma_start(fix[:, g, :], None, a["fix"],
                                            bass.IndirectOffsetOnAxis(idx_blk[:, g, NF:NF + 1], 0)
                                            ).then_inc(S["fix_in"], 16)
                if isinstance(t, int):
                    scattered(pool)
                    pool.wait_ge(S["beff_ps"], NTB)
                used = value(pool, NF * t)
                alone(pool)
                pool.wait_ge(S["bu_hi_s"], used)
                pool.wait_ge(S["bu_lo_s"], used)
                pool.wait_ge(S["ad_ps"], used)
                rows(0, 0, NF * t)
                rows(1, 1, NF * t + 1)
                if not isinstance(t, int):
                    pool.wait_ge(S["ae_s"], t + 1)
                    low(ae_lo[:], a_eff[:, :, bass.ds(t * R2, R2)], ae_hi[:], S["ae_l"])
                pool.wait_ge(S["be_s"], t + 1)
                low(be_lo[:].unsqueeze(1), b_eff[:, bass.ds(t, 1), :], be_hi[:].unsqueeze(1), S["be_l"])

            open_block(0)
            pool.wait_ge(S["wf_hi_s"], 1)
            low(wf_lo[:], wf_raw[:], wf_hi[:], S["wf_lo_s"])
            pool.wait_ge(S["wf_hi_s"], 2)
            low(ra_lo[:], ra_raw[:], ra_hi[:], S["wf_lo_s"])
            pool.wait_ge(S["wf_hi_s"], 3)
            low(rb_lo[:], rb_raw[:], rb_hi[:], S["wf_lo_s"])

            def body(t, more):
                def low_gu(par, n):
                    pool.wait_ge(S["gu_hi_s"], n + 1)
                    low(gu_lo[:, par, :], gu_raw[:], gu_hi[:, par, :], S["gu_lo_s"])
                    pool.wait_ge(S["bu_hi_s"], n + 1)
                    low(bu_lo[:, par], ab[:, par, :, P:STAB], bu_hi[:, par], S["bu_lo_s"])

                low_gu(0, NF * t)
                pool.wait_ge(S["bd_hi_s"], t + 1)
                low(bd_lo[:], fix[:, :, 2 * D:FIX], bd_hi[:], S["bd_lo_s"])

                def step(fc, j, par):
                    n = NF * t + fc
                    if not last(fc):
                        low_gu(1 - par, n + 1)
                    pool.wait_ge(S["dn_hi_s"], n + 1)
                    low(dn_lo[:, par, :], dn_raw[:], dn_hi[:, par, :], S["dn_lo_s"])
                    if not last(fc) and not last(fc, 1):
                        used = value(pool, n + 1)
                        alone(pool)
                        pool.wait_ge(S["bu_hi_s"], used)
                        pool.wait_ge(S["bu_lo_s"], used)
                        pool.wait_ge(S["ad_ps"], used)
                        rows(fc + 2, par, n + 2)

                chunks(pool, step, 1, 2)
                if more:
                    open_block(t + 1)
                for o in range(C):
                    pool.wait_ge(S["out_v"], C * t + o + 1)
                    pool.tensor_tensor(ob[:, o, :], ob[:, o, :], x1_lo[:, o, :], ALU.add).then_inc(S["out_f"], 1)
                done = value(pool, C * (t + 1))
                alone(pool)
                pool.wait_ge(S["out_f"], done)
                pool.dma_start(out[bass.ds(t, 1), :, :].rearrange("t p (c n) -> (t p) c n", c=C), ob[:]
                               ).then_inc(S["out_st"], 16)

            token_blocks(pool, body)
            pool.wait_ge(S["out_st"], 16 * NTB)

        @block.scalar
        def _(act):
            def high(dst, x, s):
                act.activation(dst, x, ACT.Copy).then_inc(s, 1)

            act.wait_ge(S["small_in"], 80)
            high(sh_hi[:], sh[:], S["prep_hi"])
            act.wait_ge(S["gsel_f"], 1)
            high(g_hi[:], gsel[:], S["prep_hi"])
            act.wait_ge(S["lora_in"], 16)
            high(la_hi[:], lora_a[:], S["lora_hi_s"])

            def high_w(e):
                act.wait_ge(S[f"w_in{e % 2}"], 16 * (e // 2 + 1))
                high(w_hi[:, e, :], w_raw[:, e, :], S["w_hi_s"])

            high_w(0)
            act.wait_ge(S["kern_f"], C)
            high(k_hi[:], kraw[:], S["kern_hi"])
            for e in range(1, PREP_AT):
                high_w(e)
            for j in range(2):
                act.wait_ge(S["aeff_ps"], j + 1)
                act.activation(a_eff[:, 2 * j:2 * j + 2, :],
                               (psG if j == 0 else psU)[:].rearrange("p (c n) -> p c n", c=2), ACT.Copy
                               ).then_inc(S["aeff_done"], 1)
            for e in range(PREP_AT, N_COND):
                high_w(e)

            def high_xs(b, ring, i, j):
                par = ring % 2
                act.wait_ge(S[f"xs_ps{ring}"], i + 1)
                act.wait_ge(S[f"h_ps{par}"], j)
                high(xs_hi[:, par, :], (psG, psU)[par][:], S[f"xs_hi{par}"])

            blocks(act, high_xs)
            act.wait_ge(S["lora_b_in"], 16)
            for ring in range(RING):
                act.wait_ge(S[f"xs_ps{ring}"], -(-(NBLK - ring) // RING))
            high(lb_hi[:], lora_b[:], S["lb_hi_s"])
            multiplied(act)
            act.wait_ge(S["late_in"], 48)
            high(ae_hi[:], a_eff[:, :, 0:R2], S["ae_s"])
            high(wf_hi[:], wf_raw[:], S["wf_hi_s"])
            high(ra_hi[:], ra_raw[:], S["wf_hi_s"])
            high(rb_hi[:], rb_raw[:], S["wf_hi_s"])

            def high_h0(t):
                act.wait_ge(S["lin_ps"], t)
                for c in range(C):
                    act.wait_ge(S["h0t_ps"], C * t + c + 1)
                    high(ht_hi[:, c, :], H0_BANK[c][:], S["h0t_hi"])

            high_h0(0)
            act.wait_ge(S["beff_ps"], NTB)
            for j in range(NTB):
                act.activation(b_eff[:, j, :], psD[0:R2, j, :], ACT.Copy).then_inc(S["beff_done"], 1)
            act.wait_ge(S["beff_done"], 1)
            high(be_hi[:], b_eff[:, 0, :], S["be_s"])

            def body(t, more):
                act.wait_ge(S["t0_m"], t + 1)
                high(r64_hi[:], r64[:], S["t0_hi"])

                def high_gu(par, n, free, gathers):
                    act.wait_ge(S["gu_in"], 16 * (n + 1))
                    act.wait_ge(S["up_ps"], free)
                    high(gu_hi[:, par, :], gu_raw[:], S["gu_hi_s"])
                    act.wait_ge(S[f"ab_in{par}"], 16 * NGT * gathers)
                    high(bu_hi[:, par], ab[:, par, :, P:STAB], S["bu_hi_s"])

                high_gu(0, NF * t, NF * t, (NF // 2 + 1) * t + 1)
                act.wait_ge(S["fix_in"], 16 * NGT * (t + 1))
                act.wait_ge(S["h_ps"], C * t)
                high(bd_hi[:], fix[:, :, 2 * D:FIX], S["bd_hi_s"])
                for o in range(C):
                    act.wait_ge(S["x1_f"], C * t + o + 1)
                    high(x1_hi[:, o, :], tokf[:, o, :], S["x1_hi_s"])
                    if o < 2:
                        act.wait_ge(S["at_ps"], 4 * t + o + 1)
                        high(at_hi[:, o, :], A_BANK[o][:], S["at_hi_s"])
                act.wait_ge(S["tg_ps"], 2 * t + 1)
                act.wait_ge(S["at_ps"], 4 * t + 3)
                high(at_hi[:, 0, :], A_BANK[2][:], S["at_hi_s"])
                act.wait_ge(S["out_st"], 16 * t)
                act.wait_ge(S["tg_m"], 2 * t + 1)
                high(tg_hi[:, 0, :], tm[:], S["tg_hi_s"])
                act.wait_ge(S["at_ps"], 4 * t + 4)
                high(at_hi[:, 1, :], A_BANK[3][:], S["at_hi_s"])

                def step(fc, j, par):
                    n = NF * t + fc
                    first = isinstance(fc, int) and fc == 0
                    if not last(fc):
                        high_gu(1 - par, n + 1, n, (NF // 2 + par) * t + j + par + 1)
                    if first:
                        act.wait_ge(S["tg_m"], 2 * t + 2)
                        high(tg_hi[:, 1, :], tm[:], S["tg_hi_s"])
                    act.wait_ge(S["ad_ps"], n + 1)
                    act.wait_ge(S["dn_ps"], n if first else n - 1)
                    high(ad_hi[:, par, :], psX[:, 0:NGT * P], S["ad_hi_s"])
                    act.wait_ge(S["dn_in"], 16 * (n + 1))
                    high(dn_hi[:, par, :], dn_raw[:], S["dn_hi_s"])
                    act.wait_ge(S["gate_ps"], n + 1)
                    act.wait_ge(S["act_f_s"], n)
                    act.activation(silu[:], psG[:], ACT.Silu).then_inc(S["silu_s"], 1)
                    act.wait_ge(S["act_f_s"], n + 1)
                    high(act_hi[:, par, :], act_f[:], S["act_hi_s"])

                chunks(act, step, 1, 1)

                act.wait_ge(S["td_m"], t + 1)
                high(td_hi[:], tm[:], S["td_hi_s"])
                for o in range(C):
                    act.wait_ge(S["h_ps"], C * t + o + 1)
                    high(ht_hi[:, o, :], psD[:, o, :], S["h_hi_s"])
                if more:
                    high(ae_hi[:], a_eff[:, :, bass.ds((t + 1) * R2, R2)], S["ae_s"])
                act.wait_ge(S["r_ps"], t + 1)
                act.activation(scores[RMAX:RS, :], psX[RMAX:RS, :], ACT.Identity,
                               bias=bias[RMAX:RS, 2 * C:2 * C + 1]).then_inc(S["r_sb"], 1)
                act.activation(scores[0:RMAX, :], psX[0:RMAX, :], ACT.Copy).then_inc(S["r_sb"], 1)
                if more:
                    high(be_hi[:].unsqueeze(1), b_eff[:, bass.ds(t + 1, 1), :], S["be_s"])
                act.wait_ge(S["sc_v"], t + 1)
                act.activation(soft[:, 2], soft[:, 1], ACT.Exp).then_inc(S["exp_s"], 1)
                act.wait_ge(S["xa_m"], t + 1)
                high(r64_hi[:], r64[:], S["xa_hi"])
                if more:
                    high_h0(t + 1)

            token_blocks(act, body)

        @block.vector
        def _(dve):
            def low(dst, x, hi, s):
                dve.tensor_tensor(dst, x, hi, ALU.subtract).then_inc(s, 1)

            done = [0]

            def then(ins):
                done[0] += 1
                ins.then_inc(S["sort_v"], 1)
                dve.wait_ge(S["sort_v"], done[0])

            dve.wait_ge(S["const_in"], 16)
            dve.wait_ge(S["small_in"], 80)
            then(dve.tensor_copy(ids0f[:], ids0[:]))
            dve.tensor_scalar(onehot[:], cst("adapter_no", ITEMS), ids0f[:], None, ALU.is_equal
                              ).then_inc(S["ids_f"], 1)
            then(dve.tensor_copy(ids1f[:], ids1[:]))
            then(dve.tensor_scalar(idx_base[:], ids1f[:], float(RANK1), cst("rank_row"), ALU.mult, ALU.add))
            dve.tensor_tensor(idx_tab[:], idx_base[:].unsqueeze(2).broadcast_to([P, GROUPS, NF + 1]),
                              cst("chunk_row").unsqueeze(1).broadcast_to([P, GROUPS, NF + 1]), ALU.add
                              ).then_inc(S["idx_tab_ready"], 1)
            dve.wait_ge(S["sort_ps1"], 1)
            then(dve.tensor_tensor(over[:], psX[0:ITEMS, N_COND:2 * N_COND].unsqueeze(2)
                                   .broadcast_to([ITEMS, N_COND, ITEMS // BI]),
                                   cst("fours", ITEMS).unsqueeze(1).broadcast_to([ITEMS, N_COND, ITEMS // BI]),
                                   ALU.is_gt))
            then(dve.tensor_reduce(nblk[:], over[:], AX.X, ALU.add))
            then(dve.tensor_tensor(earlier[:], nblk[:].unsqueeze(1).broadcast_to([ITEMS, N_COND, N_COND]),
                                   cst("earlier", ITEMS).rearrange("p (a b) -> p a b", a=N_COND), ALU.mult))
            then(dve.tensor_reduce(start[:], earlier[:], AX.X, ALU.add))
            then(dve.scalar_tensor_tensor(out=place[:], in0=start[:], scalar=float(BI), in1=psX[0:ITEMS, 0:N_COND],
                                          op0=ALU.mult, op1=ALU.add))
            then(dve.tensor_tensor(own[:], place[:], onehot[:], ALU.mult))
            then(dve.tensor_reduce(slot[:], own[:], AX.X, ALU.add))
            then(dve.tensor_scalar(perm[:], cst("slot_no", ITEMS), slot[:], None, ALU.is_equal))
            dve.wait_ge(S["lora_hi_s"], 1)
            low(la_lo[:], lora_a[:], la_hi[:], S["lora_lo_s"])
            dve.wait_ge(S["sort_ps2"], 1)
            dve.tensor_copy(blk_adp[:], psX[0:1, 2 * SLOTS:3 * SLOTS])
            then(dve.tensor_copy(item_g[:], psX[:, 0:SLOTS]))
            then(dve.tensor_scalar(empty[:], psX[:, SLOTS:2 * SLOTS], -1.0, 1.0, ALU.mult, ALU.add))
            then(dve.tensor_tensor(dummy[:], empty[:], cst("dummy"), ALU.mult))
            then(dve.tensor_tensor(item_s[:], item_g[:], dummy[:], ALU.add))
            quad = cst("quadrant").unsqueeze(1).broadcast_to([P, NBLK, BI])
            dve.tensor_tensor(sel_g[:], item_g[:].rearrange("p (b j) -> p b j", j=BI), quad, ALU.mult)
            then(dve.tensor_tensor(sel_s[:], item_s[:].rearrange("p (b j) -> p b j", j=BI), quad, ALU.mult))
            dve.tensor_reduce(row_g[:], sel_g[:], AX.X, ALU.add)
            then(dve.tensor_reduce(row_s[:], sel_s[:], AX.X, ALU.add))
            dve.tensor_scalar(idx_g[:], row_g[:], float(ITEM_T), cst("row_in_item"), ALU.mult, ALU.add)
            dve.tensor_scalar(idx_s[:], row_s[:], float(ITEM_T), cst("row_in_item"), ALU.mult, ALU.add
                              ).then_inc(S["idx_ready"], 1)
            dve.wait_ge(S["kraw_in"], 16)
            for c in range(C):
                dve.wait_ge(S["kern_ps"], c + 1)
                dve.tensor_tensor(kraw[:, c, :], psD[:, c, :], kraw[:, c, :], ALU.add).then_inc(S["kern_f"], 1)
            for e in range(N_COND):
                dve.wait_ge(S["w_hi_s"], e + 1)
                low(w_lo[:, e, :], w_raw[:, e, :], w_hi[:, e, :], S["w_lo_s"])

            def low_xs(b, ring, i, j):
                par = ring % 2
                dve.wait_ge(S[f"xs_hi{par}"], j + 1)
                low(xs_lo[:, par, :], (psG, psU)[par][:], xs_hi[:, par, :], S[f"xs_lo{par}"])

            def low_and_out(b, ring, i, j):
                low_xs(b, ring, i, j)
                evacuate(b - 1, (ring - 1) % RING, 0, j - 1 + ring % 2)

            def evacuate(b, ring, i, j):
                par = ring % 2
                dve.wait_ge(S[f"h_ps{par}"], j + 1)
                dve.wait_ge(S[f"h_st{par}"], 16 * j)
                dve.tensor_copy(h0[:, par, :], (psT, psX)[par][:]).then_inc(S[f"h_out{par}"], 1)

            low_xs(0, 0, 0, 0)
            blocks(dve, low_and_out, 1)
            evacuate(NBLK - 1, (NBLK - 1) % RING, 0, (NBLK - 1) // 2)
            dve.wait_ge(S["lb_hi_s"], 1)
            low(lb_lo[:], lora_b[:], lb_hi[:], S["lb_lo_s"])

            def low_h0(t, c):
                dve.wait_ge(S["h0t_hi"], C * t + c + 1)
                low(ht_lo[:, c, :], H0_BANK[c][:], ht_hi[:, c, :], S["h0t_lo"])

            for c in range(C):
                low_h0(0, c)

            def body(t, more):
                def low_at(k):
                    dve.wait_ge(S["at_hi_s"], 4 * t + k + 1)
                    low(at_lo[:, k % 2, :], A_BANK[k][:], at_hi[:, k % 2, :], S["at_lo_s"])

                dve.wait_ge(S["t0_ps"], t + 1)
                dve.tensor_tensor(r64[:], psX[0:R2, :], cst("group_mask", R2), ALU.mult).then_inc(S["t0_m"], 1)
                dve.wait_ge(S["t0_hi"], t + 1)
                low(r64_lo[:], r64[:], r64_hi[:], S["t0_lo"])

                dve.wait_ge(S["x_in"], 16 * (t + 1))
                dve.wait_ge(S["out_f"], C * t)
                for o in range(C):
                    dve.wait_ge(S["x1_ps"], C * t + o + 1)
                    dve.scalar_tensor_tensor(out=tokf[:, o, :], in0=psD[:, o, :], scalar=bias[:, o:o + 1],
                                             in1=tokf[:, o, :], op0=ALU.add, op1=ALU.add).then_inc(S["x1_f"], 1)
                    dve.wait_ge(S["x1_hi_s"], C * t + o + 1)
                    low(x1_lo[:, o, :], tokf[:, o, :], x1_hi[:, o, :], S["x1_lo_s"])
                    if o < 2:
                        low_at(o)

                def masked(ps, s):
                    dve.tensor_tensor(tm[:].rearrange("p (g n) -> p g n", g=NGT),
                                      ps.rearrange("p (g n) -> p g n", g=NGT),
                                      cst("item_mask").unsqueeze(1).broadcast_to([P, NGT, GT]),
                                      ALU.mult).then_inc(s, 1)

                def ranks(k):
                    dve.wait_ge(S["tg_ps"], 2 * t + k + 1)
                    masked(psD[:, k, :], S["tg_m"])
                    if k == 0:
                        low_at(2)
                    dve.wait_ge(S["tg_hi_s"], 2 * t + k + 1)
                    low(tg_lo[:, k, :], tm[:], tg_hi[:, k, :], S["tg_lo_s"])

                ranks(0)
                low_at(3)
                dve.wait_ge(S["tg_lo_s"], 2 * t + 1)
                ranks(1)

                def step(fc, j, par):
                    n = NF * t + fc
                    dve.wait_ge(S["ad_hi_s"], n + 1)
                    low(ad_lo[:, par, :], psX[:, 0:NGT * P], ad_hi[:, par, :], S["ad_lo_s"])
                    dve.wait_ge(S["silu_s"], n + 1)
                    dve.wait_ge(S["up_ps"], n + 1)
                    dve.wait_ge(S["act_lo_s"], n)
                    dve.tensor_tensor(act_f[:], psU[:], silu[:], ALU.mult).then_inc(S["act_f_s"], 1)
                    dve.wait_ge(S["act_hi_s"], n + 1)
                    low(act_lo[:, par, :], act_f[:], act_hi[:, par, :], S["act_lo_s"])

                chunks(dve, step, 0, 1)

                dve.wait_ge(S["td_ps"], NF * (t + 1))
                dve.wait_ge(S["tg_lo_s"], 2 * (t + 1))
                masked(psT[:], S["td_m"])
                dve.wait_ge(S["td_hi_s"], t + 1)
                low(td_lo[:], tm[:], td_hi[:], S["td_lo_s"])
                for o in range(C):
                    dve.wait_ge(S["h_hi_s"], C * t + o + 1)
                    low(ht_lo[:, o, :], psD[:, o, :], ht_hi[:, o, :], S["h_lo_s"])

                links = [0]

                def link(ins):
                    links[0] += 1
                    ins.then_inc(S["soft_v"], 1)
                    dve.wait_ge(S["soft_v"], LINKS * t + links[0])

                sc = soft[:, 0]
                e = soft[:, 2]
                prob = soft[:, 3]
                dve.wait_ge(S["sc_ps"], t + 1)
                link(dve.tensor_copy(sc, psG[:, 0:SUB * NR].rearrange("p (s r) -> p s r", s=SUB)))
                link(dve.tensor_reduce(soft[:, 4, :, 0], sc, AX.X, ALU.max))
                dve.tensor_tensor(soft[:, 1], sc, soft[:, 4, :, 0:1].broadcast_to([P, SUB, NR]), ALU.subtract
                                  ).then_inc(S["sc_v"], 1)
                dve.wait_ge(S["exp_s"], t + 1)
                link(dve.tensor_reduce(soft[:, 5, :, 0], e, AX.X, ALU.add))
                link(dve.reciprocal(soft[:, 5, :, 1], soft[:, 5, :, 0]))
                link(dve.tensor_tensor(prob, e, soft[:, 5, :, 1:2].broadcast_to([P, SUB, NR]), ALU.mult))
                link(dve.tensor_reduce(soft[:, 6, :, 0], prob, AX.X, ALU.max))
                link(dve.reciprocal(soft[:, 6, :, 1], soft[:, 6, :, 0]))
                dve.tensor_tensor(soft[:, 7, :, 0], soft[:, 6, :, 0], soft[:, 6, :, 1], ALU.mult)
                link(dve.tensor_tensor(soft[:, 8], prob, soft[:, 6, :, 0:1].broadcast_to([P, SUB, NR]), ALU.is_ge))
                link(dve.tensor_scalar(soft[:, 9], soft[:, 8], -1.0, 1.0, ALU.mult, ALU.add))
                link(dve.tensor_copy(soft[:, 10, :, 0], soft[:, 7, :, 0]))
                for k in range(1, NR):
                    link(dve.tensor_tensor(soft[:, 10, :, k], soft[:, 10, :, k - 1], soft[:, 9, :, k - 1], ALU.mult))
                assert links[0] == LINKS
                lo = 0
                dve.wait_ge(S["mask_ps"], SUB * t)
                for k, hi in enumerate(RANKS):
                    last = dve.tensor_copy(mexp[:, :, lo:hi],
                                           soft[:, 10, :, k:k + 1].broadcast_to([P, SUB, hi - lo]))
                    lo = hi
                    last.then_inc(S["mexp_s"], 1)
                dve.wait_ge(S["mask_ps"], SUB * (t + 1))
                dve.wait_ge(S["r_sb"], 2 * (t + 1))
                dve.tensor_tensor(r64[:], psU[0:RMAX, :], scores[0:RMAX, :], ALU.mult).then_inc(S["xa_m"], 1)
                dve.wait_ge(S["xa_hi"], t + 1)
                low(r64_lo[:], r64[:], r64_hi[:], S["xa_lo"])

                def first_sum(o):
                    dve.wait_ge(S["out_ps"], C * t + o + 1)
                    dve.scalar_tensor_tensor(out=ob[:, o, :], in0=psD[:, o, :], scalar=bias[:, C + o:C + o + 1],
                                             in1=x1_hi[:, o, :], op0=ALU.add, op1=ALU.add).then_inc(S["out_v"], 1)

                for c in range(C):
                    if more:
                        low_h0(t + 1, c)
                    if c:
                        first_sum(c - 1)
                first_sum(C - 1)

            token_blocks(dve, body)

        @block.tensor
        def _(pe):
            ident = cst("ident")

            def product(ps, w, x, start, stop):
                (wh, wl), (xh, xl) = w, x
                pe.matmul(ps, wh, xh, start=start, stop=False, skip_group_check=True)
                pe.matmul(ps, wh, xl, start=False, stop=False, skip_group_check=True)
                return pe.matmul(ps, wl, xh, start=False, stop=stop, skip_group_check=True)

            def both(hi, lo, *ix):
                return hi[ix], lo[ix]

            al = slice(None)
            pe.wait_ge(S["const_in"], 16)
            pe.wait_ge(S["ids_f"], 1)
            pe.matmul(psX[0:ITEMS, 0:N_COND], cst("before", ITEMS), onehot[:], start=True, stop=True)
            pe.matmul(psX[0:ITEMS, N_COND:2 * N_COND], cst("ones", ITEMS)[:, 0:ITEMS], onehot[:],
                      start=True, stop=True).then_inc(S["sort_ps1"], 1)
            pe.wait_ge(S["sort_v"], 11)
            pe.matmul(psX[:, 0:SLOTS], cst("item_no", ITEMS), perm[:], start=True, stop=True)
            pe.matmul(psX[:, SLOTS:2 * SLOTS], cst("ones", ITEMS), perm[:], start=True, stop=True)
            pe.matmul(psX[0:1, 2 * SLOTS:3 * SLOTS], ids0f[:], perm[:], start=True, stop=True
                      ).then_inc(S["sort_ps2"], 1)
            pe.wait_ge(S["sh_lo_s"], 1)
            for c in range(C):
                product(psD[:, c, :], both(sh_hi, sh_lo, al, 0, slice(c * P, c * P + P)),
                        both(sh_hi, sh_lo, al, 1, al), True, True).then_inc(S["kern_ps"], 1)
            pe.wait_ge(S["g_lo_s"], 1)
            pe.wait_ge(S["lora_lo_s"], 1)
            for c in range(C):
                ps = (psG, psU)[c // 2][:, (c % 2) * 256:(c % 2) * 256 + 256]
                for k in range(4):
                    mm = product(ps, both(la_hi, la_lo, al, k, slice(c * P, c * P + P)),
                                 both(g_hi, g_lo, al, k, al), k == 0, k == 3)
                if c % 2:
                    mm.then_inc(S["aeff_ps"], 1)
            def turn(b, ring, i, j):
                par = ring % 2
                pe.wait_ge(S[f"xs_in{ring}"], 16 * (i + 1))
                pe.wait_ge(S[f"xs_lo{par}"], j)
                for c in range(C):
                    mm = pe.transpose((psG, psU)[par][:, c * P:c * P + P], xs[:, ring, c * P:c * P + P], ident)
                mm.then_inc(S[f"xs_ps{ring}"], 1)

            def cond(b, ring, i, j):
                par = ring % 2
                e = pe.value_load(blk_adp[0:1, bass.ds(b * BI, 1)], min_val=0, max_val=N_COND - 1)
                pe.wait_ge(S[f"xs_lo{par}"], j + 1)
                pe.wait_ge(S[f"h_out{par}"], j)
                ps = (psT, psX)[par][:]
                for c in range(C):
                    w = [v[:, bass.ds(e, 1), c * D:(c + 1) * D].rearrange("p e n -> p (e n)") for v in (w_hi, w_lo)]
                    xh, xl = xs_hi[:, par, c * P:c * P + P], xs_lo[:, par, c * P:c * P + P]
                    pe.matmul(ps, xh, w[0], start=c == 0, stop=False)
                    pe.matmul(ps, xl, w[0], start=False, stop=False)
                    mm = pe.matmul(ps, xh, w[1], start=False, stop=c == C - 1)
                mm.then_inc(S[f"h_ps{par}"], 1)

            def turn_and_cond(b, ring, i, j):
                turn(b, ring, i, j)
                cond(b - 1, (ring - 1) % RING, 0, j - 1 + ring % 2)

            pe.wait_ge(S["aeff_done"], 2)
            pe.wait_ge(S["idx_ready"], 1)
            turn(0, 0, 0, 0)
            pe.wait_ge(S["w_lo_s"], N_COND)
            blocks(pe, turn_and_cond, 1)
            cond(NBLK - 1, (NBLK - 1) % RING, 0, (NBLK - 1) // 2)
            def b_gated(j):
                for k in range(4):
                    mm = product(psD[0:R2, j, :], both(g_hi, g_lo, al, k, slice(j * R2, (j + 1) * R2)),
                                 both(lb_hi, lb_lo, al, k, al), k == 0, k == 3)
                mm.then_inc(S["beff_ps"], 1)

            pe.wait_ge(S["lb_lo_s"], 1)
            pe.wait_ge(S["kern_f"], C)
            for j in range(NTB - 1):
                b_gated(j)
            for par in range(2):
                pe.wait_ge(S[f"h_out{par}"], NBLK // 2)

            def turn_h0(t):
                pe.wait_ge(S["h0_in"], 16 * (t + 1))
                pe.wait_ge(S["r_sb"], 2 * t)
                pe.wait_ge(S["td_m"], t)
                for c in range(C):
                    if c == C - 1:
                        pe.wait_ge(S["xa_m"], t)
                    for s in range(SUB):
                        mm = pe.transpose(H0_BANK[c][:, s * P:s * P + P], tok[:, s, c * P:c * P + P], ident)
                    mm.then_inc(S["h0t_ps"], 1)

            turn_h0(0)
            b_gated(NTB - 1)

            def body(t, more):
                def turn_a(k):
                    ps = A_BANK[k]
                    for c in range(C):
                        at = (k // 2) * D + c * P
                        mm = pe.transpose(ps[:, c * P:c * P + P], fix[:, k % 2, at:at + P], ident)
                    mm.then_inc(S["at_ps"], 1)

                pe.wait_ge(S["ae_l"], t + 1)
                for c in range(C):
                    pe.wait_ge(S["h0t_lo"], C * t + c + 1)
                    mm = product(psX[0:R2, :], both(ae_hi, ae_lo, al, c, al), both(ht_hi, ht_lo, al, c, al),
                                 c == 0, c == C - 1)
                mm.then_inc(S["t0_ps"], 1)
                pe.wait_ge(S["out_v"], C * t)
                pe.wait_ge(S["beff_done"], NTB)
                for o in range(C):
                    for c in range(C):
                        product(psD[:, o, :], both(k_hi, k_lo, al, c, slice(o * P, o * P + P)),
                                both(ht_hi, ht_lo, al, c, al), c == 0, False)
                    if o == 0:
                        pe.wait_ge(S["be_l"], t + 1)
                        pe.wait_ge(S["t0_lo"], t + 1)
                    product(psD[:, o, :], both(be_hi, be_lo, al, slice(o * P, o * P + P)),
                            (r64_hi[:], r64_lo[:]), False, True).then_inc(S["x1_ps"], 1)
                    if o < 2:
                        pe.wait_ge(S["fix_in"], 16 * NGT * (t + 1))
                        turn_a(o)

                def ranks(k):
                    pe.wait_ge(S["at_lo_s"], 4 * t + 2 * k + 2)
                    for cs in ((0, 1, 2), (3,)):
                        for g in range(NGT):
                            cols = slice(g * GT, g * GT + GT)
                            for c in cs:
                                if k == 0 and g == 0:
                                    pe.wait_ge(S["x1_lo_s"], C * t + c + 1)
                                mm = product(psD[:, k, cols], both(at_hi, at_lo, al, g, slice(c * P, c * P + P)),
                                             both(x1_hi, x1_lo, al, c, cols), g == 0 and c == 0, c == C - 1)
                    mm.then_inc(S["tg_ps"], 1)

                ranks(0)
                turn_a(2)
                turn_a(3)

                def down(par, n, opens, closes):
                    pe.wait_ge(S["act_hi_s"], n)
                    pe.wait_ge(S["act_lo_s"], n)
                    pe.wait_ge(S["ad_lo_s"], n)
                    for g in range(NGT):
                        cols = slice(g * GT, g * GT + GT)
                        mm = product(psT[:, cols], both(ad_hi, ad_lo, al, par, slice(g * P, g * P + P)),
                                     both(act_hi, act_lo, al, par, cols), opens and g == 0, closes)
                    mm.then_inc(S["td_ps"], 1)
                    pe.wait_ge(S["dn_lo_s"], n)
                    for o in range(C):
                        mm = product(psD[:, o, :], both(dn_hi, dn_lo, al, par, slice(o * P, o * P + P)),
                                     both(act_hi, act_lo, al, par, al), opens, False)
                    mm.then_inc(S["dn_ps"], 1)

                def step(fc, j, par):
                    n = NF * t + fc
                    first = isinstance(fc, int) and fc == 0

                    def turn_down():
                        pe.wait_ge(S["ad_lo_s"], n)
                        for g in range(NGT):
                            mm = pe.transpose(psX[:, g * P:g * P + P], ab[:, par, g, 0:P], ident)
                        mm.then_inc(S["ad_ps"], 1)

                    def gate_or_up(k, ps):
                        for c in range(C):
                            at = k * D + c * P
                            product(ps[:], both(gu_hi, gu_lo, al, par, slice(at, at + P)),
                                    both(x1_hi, x1_lo, al, c, al), c == 0, False)

                    pe.wait_ge(S["bu_hi_s"], n + 1)
                    if not first:
                        turn_down()
                    pe.wait_ge(S["gu_lo_s"], n + 1)
                    pe.wait_ge(S["silu_s"], n)
                    gate_or_up(0, psG)
                    if first:
                        ranks(1)
                        turn_down()
                    pe.wait_ge(S["act_f_s"], n)
                    gate_or_up(1, psU)
                    if first:
                        pe.wait_ge(S["tg_lo_s"], 2 * t + 2)
                    pe.wait_ge(S["bu_lo_s"], n + 1)
                    for k, (ps, s) in enumerate(((psG, "gate_ps"), (psU, "up_ps"))):
                        for g in range(NGT):
                            cols = slice(g * GT, g * GT + GT)
                            mm = product(ps[:, cols], both(bu_hi, bu_lo, al, par, g, slice(k * P, k * P + P)),
                                         both(tg_hi, tg_lo, al, k, cols), False, True)
                        mm.then_inc(S[s], 1)
                    if not first:
                        down(1 - par, n, isinstance(fc, int) and fc == 1, False)

                chunks(pe, step, 2, 1)
                down((NF - 1) % 2, NF * (t + 1), False, True)

                pe.wait_ge(S["td_hi_s"], t + 1)
                pe.wait_ge(S["td_lo_s"], t + 1)
                pe.wait_ge(S["bd_lo_s"], t + 1)
                for o in range(C):
                    for g in range(NGT):
                        cols = slice(g * GT, g * GT + GT)
                        mm = product(psD[:, o, cols], both(bd_hi, bd_lo, al, g, slice(o * P, o * P + P)),
                                     both(td_hi, td_lo, al, cols), False, True)
                    mm.then_inc(S["h_ps"], 1)
                pe.wait_ge(S["wf_lo_s"], 3)
                for c in range(C):
                    pe.wait_ge(S["h_lo_s"], C * t + c + 1)
                    mm = product(psX[0:RS, :], both(ra_hi, ra_lo, al, c, al), both(ht_hi, ht_lo, al, c, al),
                                 c == 0, c == C - 1)
                mm.then_inc(S["r_ps"], 1)

                def linear(o):
                    for c in range(C):
                        mm = product(psD[:, o, :], both(wf_hi, wf_lo, al, c, slice(o * P, o * P + P)),
                                     both(ht_hi, ht_lo, al, c, al), c == 0, False)
                    return mm

                linear(0)
                count = value(pe, 2 * t + 1)
                alone(pe)
                pe.wait_ge(S["r_sb"], count)
                for s in range(SUB):
                    mm = pe.transpose(psG[:, s * NR:(s + 1) * NR], scores[RMAX:RS, s * P:(s + 1) * P],
                                      const[RMAX:RS, RMAX:RS])
                mm.then_inc(S["sc_ps"], 1)
                linear(1)
                linear(2)
                count = value(pe, NR * (t + 1))
                alone(pe)
                pe.wait_ge(S["mexp_s"], count)
                for s in range(SUB):
                    pe.transpose(psU[0:RMAX, s * P:(s + 1) * P], mexp[:, s, :], ident).then_inc(S["mask_ps"], 1)
                linear(3).then_inc(S["lin_ps"], 1)
                if more:
                    turn_h0(t + 1)
                pe.wait_ge(S["xa_lo"], t + 1)
                for o in range(C):
                    product(psD[:, o, :], both(rb_hi, rb_lo, al, slice(o * P, o * P + P)),
                            (r64_hi[:], r64_lo[:]), False, True).then_inc(S["out_ps"], 1)

            token_blocks(pe, body)


def kernel(**inputs):
    import concourse.bacc as bacc
    from concourse.bass_utils import run_bass_kernel_spmd as run

    v = {k: np.asarray(x) for k, x in inputs.items()}

    def features(w):
        *rest, f, n = w.shape
        return np.moveaxis(w.reshape(*rest, f // P, P, n), -3, -2)

    def padded(w, axis):
        width = [(0, 0)] * w.ndim
        width[axis] = (0, NF * P - F)
        return np.pad(w, width)

    x = v["x"].reshape(TOKENS, D)
    bias = np.zeros((P, 2 * C + 1), np.float32)
    bias[:, 0:C] = v["L0_ffn_bias"].reshape(C, P).T
    bias[:, C:2 * C] = v["L1_ffn_b"].reshape(C, P).T
    bias[RMAX:RMAX + NR, 2 * C] = v["L1_ffn_gate_b"]
    gate = v["L0_ffn_gate"].reshape(GROUPS, 4, N_LORA // 4)
    gu = np.stack([padded(v["L1_cond_W_gate"], 0), padded(v["L1_cond_W_up"], 0)])
    gu = gu.reshape(2, NF, P, C, P).transpose(1, 4, 0, 3, 2)
    dn = padded(v["L1_cond_W_down"], 1).reshape(D, NF, P).transpose(1, 2, 0)
    ab = np.stack([
        padded(v["L1_cond_A_down"][0], 2),
        padded(v["L1_cond_B_gate"][0], 1).transpose(0, 2, 1),
        padded(v["L1_cond_B_up"][0], 1).transpose(0, 2, 1),
    ]).reshape(3, N_ADP * RANK1, NF, P).transpose(2, 1, 0, 3)
    fix = np.stack([v["L1_cond_A_gate"][0], v["L1_cond_A_up"][0], v["L1_cond_B_down"][0].transpose(0, 2, 1)], 2)
    arrays = {
        "x": x,
        "x_t": x.reshape(NTB, TB, C, P).transpose(0, 3, 2, 1).reshape(NTB, P, C * TB),
        "const": constants(),
        "ids0": v["itok_B_3_7"].reshape(ITEMS, 1),
        "ids1": np.repeat(v["itok_B_2_6"].reshape(ITEMS // GI, GI), RANK1, 1).T,
        "gate": np.repeat(gate.transpose(2, 1, 0), RANK0, 0),
        "bias": bias,
        "shared": np.stack([v["L0_ffn_lora_A_shared"], v["L0_ffn_lora_B_shared"].T], 1),
        "lora_a": v["L0_ffn_lora_A"].reshape(4, P, D).transpose(1, 0, 2),
        "lora_b": v["L0_ffn_lora_B"].transpose(0, 2, 1).reshape(4, P, D).transpose(1, 0, 2),
        "kern": features(v["L0_ffn_kernel"]),
        "cond_w": features(v["L0_cond_weight"].transpose(0, 2, 1)).reshape(N_COND, P, C * D),
        "wf": features(v["L1_ffn_W"].T),
        "ra": features(np.concatenate([v["L1_ffn_A"].T, v["L1_ffn_gate_w"].T], 1)),
        "rb": v["L1_ffn_B"].T,
        "gu": gu.reshape(NF, P, 2 * D),
        "dn": dn,
        "ab": ab.reshape(NF * N_ADP * RANK1, STAB),
        "fix": fix.reshape(N_ADP * RANK1, FIX),
    }
    arrays = {"in_" + k: np.ascontiguousarray(w) for k, w in arrays.items()}
    nc = bacc.Bacc("TRN2", target_bir_lowering=False, num_devices=1)
    drams = {k[3:]: nc.dram_tensor(k, w.shape, mybir.dt.from_np(w.dtype), kind="ExternalInput").ap()
             for k, w in arrays.items()}
    out = nc.dram_tensor("out_t", (NTB, P, C * TB), F32, kind="ExternalOutput").ap()
    two_layers(nc, drams, out)
    got = run(nc, [arrays], core_ids=[0]).results[0]["out_t"]
    return got.reshape(NTB, P, C, TB).transpose(0, 3, 2, 1).reshape(ITEMS, ITEM_T, D)
```
